# Optimizing a Trainium2 kernel written in Bass

```python
import numpy as np
import jax
import jax.numpy as jnp

def _softmax(x, axis=-1):
    return jax.nn.softmax(x, axis=axis)

def _gelu(x):
    return jax.nn.gelu(x, approximate=True)

def _silu(x):
    return jax.nn.silu(x)

def _sigmoid(x):
    return jax.nn.sigmoid(x)

def _layernorm(x, axis=-1, eps=1e-05):
    m = jnp.mean(x, axis=axis, keepdims=True)
    v = jnp.var(x, axis=axis, keepdims=True)
    return (x - m) / jnp.sqrt(v + eps)

def _scatter_add(tgt, idx, src, axis=0):
    return tgt.at[idx].add(src)

def _segment_sum(src, seg, n):
    return jax.ops.segment_sum(src, seg, n)
kernel_name = 'mk_seq_preln_d2_jaxref_r8_7530a3'

def setup_inputs(seed: int=0):
    np.random.seed(seed)
    _w = jnp.asarray

    def _L0_attn_setup():
        import math
        import jax, jax.numpy as jnp
        import numpy as np
        B, S, D, H = (2, 256, 128, 16)
        HD = D // H
        key = jax.random.key(seed)
        k1, k2, k3 = jax.random.split(key, 3)
        h = jax.random.normal(k1, (B, S, D), dtype=jnp.float32)
        Wqvk = jax.random.normal(k2, (D, 3 * D), dtype=jnp.float32) * (1.0 / math.sqrt(D))
        Wo = jax.random.normal(k3, (D, D), dtype=jnp.float32) * (1.0 / math.sqrt(D))
        return {'h': h, 'Wqvk': Wqvk, 'Wo': Wo}
    _L0_attn_in = _L0_attn_setup()

    def _L0_ffn_setup():
        import jax, jax.numpy as jnp
        import numpy as np
        NUM_EXPERTS = 8
        TOP_K = 2
        B, T, D, F = (4, 256, 128, 352)
        key = jax.random.key(seed)
        ks = jax.random.split(key, 5)
        return {'x': jax.random.normal(ks[0], (B, T, D), dtype=jnp.float32), 'router_w': jax.random.normal(ks[1], (D, NUM_EXPERTS), dtype=jnp.float32) * 0.02, 'gate_proj': jax.random.normal(ks[2], (NUM_EXPERTS, D, F), dtype=jnp.float32) * 0.02, 'up_proj': jax.random.normal(ks[3], (NUM_EXPERTS, D, F), dtype=jnp.float32) * 0.02, 'down_proj': jax.random.normal(ks[4], (NUM_EXPERTS, F, D), dtype=jnp.float32) * 0.02}
    _L0_ffn_in = _L0_ffn_setup()

    def _L1_attn_setup():
        import jax, jax.numpy as jnp
        import numpy as np
        D_MODEL = 128
        N_HEADS = 16
        KV_HEADS = 4
        D_HEAD = D_MODEL // N_HEADS

        def _rope_factor(n, d_head, dtype):
            i = jnp.arange(d_head)
            theta = jnp.power(jnp.asarray(10000.0, dtype), (-2.0 * (i // 2) / d_head).astype(dtype))
            pos = jnp.arange(n, dtype=dtype)
            ang = pos[:, None] * theta[None, :]
            sign = jnp.where(jnp.arange(n) % 2 == 1, -1.0, 1.0).astype(dtype)
            return jnp.cos(ang) + sign[:, None] * jnp.sin(ang)

        def _rms_norm(x, g):
            eps = jnp.finfo(x.dtype).eps
            inv = jax.lax.rsqrt(jnp.mean(x * x, axis=-1, keepdims=True) + eps)
            return x * inv * g
        key = jax.random.key(seed)
        ks = jax.random.split(key, 5)
        s_in = 1.0 / np.sqrt(D_MODEL)
        x = jax.random.normal(ks[0], (2, 256, D_MODEL), dtype=jnp.float32)
        w_q = jax.random.normal(ks[1], (D_MODEL, D_MODEL), dtype=jnp.float32) * s_in
        w_k = jax.random.normal(ks[2], (D_MODEL, D_HEAD * KV_HEADS), dtype=jnp.float32) * s_in
        w_v = jax.random.normal(ks[3], (D_MODEL, D_HEAD * KV_HEADS), dtype=jnp.float32) * s_in
        w_o = jax.random.normal(ks[4], (D_MODEL, D_MODEL), dtype=jnp.float32) * s_in
        g = jnp.ones((D_MODEL,), dtype=jnp.float32)
        return {'x': x, 'w_q': w_q, 'w_k': w_k, 'w_v': w_v, 'w_o': w_o, 'g': g}
    _L1_attn_in = _L1_attn_setup()

    def _L1_ffn_setup():
        import jax, jax.numpy as jnp
        import numpy as np
        B, S, D_MODEL, D_FF = (4, 256, 128, 512)

        def _quantum_transform(hidden, theta, w_real, w_imag):
            imag = w_imag * jnp.sin(theta + hidden * 0.1)
            quantum_phase = jnp.cos(theta) * w_real + jnp.sin(theta) * w_imag
            return hidden + quantum_phase * imag * 0.1
        key = jax.random.key(seed)
        ks = jax.random.split(key, 8)
        return {'x': jax.random.normal(ks[0], (B, S, D_MODEL), dtype=jnp.float32), 'W1': jax.random.normal(ks[1], (D_MODEL, D_FF), dtype=jnp.float32) * (1.0 / np.sqrt(D_MODEL)), 'b1': jnp.zeros((D_FF,), dtype=jnp.float32), 'quantum_phases': jax.random.normal(ks[2], (D_FF,), dtype=jnp.float32) * (2.0 * np.pi), 'quantum_weights_real': jax.random.normal(ks[3], (D_FF,), dtype=jnp.float32) * 0.1, 'quantum_weights_imag': jax.random.normal(ks[4], (D_FF,), dtype=jnp.float32) * 0.1, 'W2': jax.random.normal(ks[5], (D_FF, D_MODEL), dtype=jnp.float32) * (1.0 / np.sqrt(D_FF)), 'b2': jnp.zeros((D_MODEL,), dtype=jnp.float32)}
    _L1_ffn_in = _L1_ffn_setup()
    _d = {'L0_attn_h': _L0_attn_in['h'], 'L0_attn_Wqvk': _L0_attn_in['Wqvk'], 'L0_attn_Wo': _L0_attn_in['Wo'], 'L0_ffn_router_w': _L0_ffn_in['router_w'], 'L0_ffn_gate_proj': _L0_ffn_in['gate_proj'], 'L0_ffn_up_proj': _L0_ffn_in['up_proj'], 'L0_ffn_down_proj': _L0_ffn_in['down_proj'], 'L1_attn_w_q': _L1_attn_in['w_q'], 'L1_attn_w_k': _L1_attn_in['w_k'], 'L1_attn_w_v': _L1_attn_in['w_v'], 'L1_attn_w_o': _L1_attn_in['w_o'], 'L1_attn_g': _L1_attn_in['g'], 'L1_ffn_W1': _L1_ffn_in['W1'], 'L1_ffn_b1': _L1_ffn_in['b1'], 'L1_ffn_quantum_phases': _L1_ffn_in['quantum_phases'], 'L1_ffn_quantum_weights_real': _L1_ffn_in['quantum_weights_real'], 'L1_ffn_quantum_weights_imag': _L1_ffn_in['quantum_weights_imag'], 'L1_ffn_W2': _L1_ffn_in['W2'], 'L1_ffn_b2': _L1_ffn_in['b2']}
    _x0 = _d['L0_attn_h']
    _d['L0_attn_h'] = jax.random.normal(jax.random.fold_in(jax.random.key(seed), 1), (4, 1024, 128), dtype=_x0.dtype)
    del _x0
    return _d

def reference(L0_attn_h, L0_attn_Wqvk, L0_attn_Wo, L0_ffn_router_w, L0_ffn_gate_proj, L0_ffn_up_proj, L0_ffn_down_proj, L1_attn_w_q, L1_attn_w_k, L1_attn_w_v, L1_attn_w_o, L1_attn_g, L1_ffn_W1, L1_ffn_b1, L1_ffn_quantum_phases, L1_ffn_quantum_weights_real, L1_ffn_quantum_weights_imag, L1_ffn_W2, L1_ffn_b2):

    def _L0_attn_ref(h, Wqvk, Wo):
        import math
        import jax, jax.numpy as jnp
        import numpy as np
        B, S, D, H = (2, 256, 128, 16)
        HD = D // H
        b, s, d = h.shape
        qvk = (h @ Wqvk).reshape(b, s, 3, H, HD)
        q, v, k = (qvk[:, :, 0], qvk[:, :, 1], qvk[:, :, 2])
        scores = jnp.einsum('bshi,bthi->bsth', q, k)
        mask = jnp.where(jnp.arange(s)[None, :] > jnp.arange(s)[:, None], jnp.float32(-jnp.inf), jnp.float32(0.0))
        scores = scores + mask[None, :, :, None]
        scores = scores / math.sqrt(d)
        weights = jax.nn.softmax(scores, axis=2)
        wv = jnp.einsum('bsth,bthi->bshi', weights, v).reshape(b, s, d)
        return wv @ Wo

    def _L0_ffn_ref(x, router_w, gate_proj, up_proj, down_proj):
        import jax, jax.numpy as jnp
        import numpy as np
        NUM_EXPERTS = 8
        TOP_K = 2
        B, T, D, F = (4, 256, 128, 352)
        scores = jnp.einsum('btd,de->bte', x, router_w).astype(jnp.float32)
        probs = jax.nn.softmax(scores, axis=-1)
        routing_weights, routing_idx = jax.lax.top_k(probs, TOP_K)
        routing_weights = (routing_weights / jnp.sum(routing_weights, axis=-1, keepdims=True)).astype(x.dtype)
        one_hot = jax.nn.one_hot(routing_idx, NUM_EXPERTS, dtype=x.dtype)
        expert_w = jnp.einsum('btke,btk->bte', one_hot, routing_weights)
        dispatched = jnp.einsum('btd,btke->bted', x, one_hot)
        gate = jnp.einsum('bted,edf->btef', dispatched, gate_proj)
        up = jnp.einsum('bted,edf->btef', dispatched, up_proj)
        acts = jax.nn.silu(gate) * up
        expert_out = jnp.einsum('btef,efd->bted', acts, down_proj)
        return jnp.einsum('bted,bte->btd', expert_out, expert_w)

    def _L1_attn_ref(x, w_q, w_k, w_v, w_o, g):
        import jax, jax.numpy as jnp
        import numpy as np
        D_MODEL = 128
        N_HEADS = 16
        KV_HEADS = 4
        D_HEAD = D_MODEL // N_HEADS

        def _rope_factor(n, d_head, dtype):
            i = jnp.arange(d_head)
            theta = jnp.power(jnp.asarray(10000.0, dtype), (-2.0 * (i // 2) / d_head).astype(dtype))
            pos = jnp.arange(n, dtype=dtype)
            ang = pos[:, None] * theta[None, :]
            sign = jnp.where(jnp.arange(n) % 2 == 1, -1.0, 1.0).astype(dtype)
            return jnp.cos(ang) + sign[:, None] * jnp.sin(ang)

        def _rms_norm(x, g):
            eps = jnp.finfo(x.dtype).eps
            inv = jax.lax.rsqrt(jnp.mean(x * x, axis=-1, keepdims=True) + eps)
            return x * inv * g
        b, n, _ = x.shape
        reps = N_HEADS // KV_HEADS
        x_norm = _rms_norm(x, g)
        q = (x_norm @ w_q).reshape(b, n, N_HEADS, D_HEAD).transpose(0, 2, 1, 3)
        k = (x_norm @ w_k).reshape(b, n, KV_HEADS, D_HEAD).transpose(0, 2, 1, 3)
        v = (x_norm @ w_v).reshape(b, n, KV_HEADS, D_HEAD).transpose(0, 2, 1, 3)
        rf = _rope_factor(n, D_HEAD, x.dtype)
        q = q * rf
        k = k * rf
        q5 = q.reshape(b, reps, KV_HEADS, n, D_HEAD)
        scale = jnp.asarray(np.sqrt(D_MODEL), x.dtype)
        qkt = jnp.einsum('brkqa,bkca->brkqc', q5, k) / scale
        attn = jax.nn.softmax(qkt, axis=-1)
        s = jnp.einsum('brkqc,bkca->brkqa', attn, v)
        s = s.reshape(b, N_HEADS, n, D_HEAD).transpose(0, 2, 1, 3).reshape(b, n, D_MODEL)
        o = s @ w_o
        return s + o

    def _L1_ffn_ref(x, W1, b1, quantum_phases, quantum_weights_real, quantum_weights_imag, W2, b2):
        import jax, jax.numpy as jnp
        import numpy as np
        B, S, D_MODEL, D_FF = (4, 256, 128, 512)

        def _quantum_transform(hidden, theta, w_real, w_imag):
            imag = w_imag * jnp.sin(theta + hidden * 0.1)
            quantum_phase = jnp.cos(theta) * w_real + jnp.sin(theta) * w_imag
            return hidden + quantum_phase * imag * 0.1
        hidden = jnp.einsum('bsd,df->bsf', x, W1) + b1
        q = _quantum_transform(hidden, quantum_phases, quantum_weights_real, quantum_weights_imag)
        act = jax.nn.relu(q)
        return jnp.einsum('bsf,fd->bsd', act, W2) + b2
    x = L0_attn_h
    x = x + _L0_attn_ref(_layernorm(x, axis=-1), L0_attn_Wqvk, L0_attn_Wo)
    x = x + _L0_ffn_ref(_layernorm(x, axis=-1), L0_ffn_router_w, L0_ffn_gate_proj, L0_ffn_up_proj, L0_ffn_down_proj)
    x = x + _L1_attn_ref(_layernorm(x, axis=-1), L1_attn_w_q, L1_attn_w_k, L1_attn_w_v, L1_attn_w_o, L1_attn_g)
    x = x + _L1_ffn_ref(_layernorm(x, axis=-1), L1_ffn_W1, L1_ffn_b1, L1_ffn_quantum_phases, L1_ffn_quantum_weights_real, L1_ffn_quantum_weights_imag, L1_ffn_W2, L1_ffn_b2)
    return x

_drawn_inputs = setup_inputs


def setup_inputs(seed=0):
    import zlib

    import numpy as np

    out = dict(_drawn_inputs(seed))
    spreads = {'L1_attn_g': (1.0, 0.6), 'L1_ffn_b1': (0.0, 0.641), 'L1_ffn_b2': (0.0, 0.406)}
    factors = {'L0_ffn_router_w': 8.0,
     'L0_ffn_gate_proj': 8.0,
     'L0_ffn_up_proj': 8.0,
     'L0_ffn_down_proj': 8.0,
     'L1_attn_w_q': 2.954,
     'L1_attn_w_k': 3.161,
     'L1_ffn_quantum_phases': 64.0,
     'L1_ffn_quantum_weights_real': 64.0,
     'L1_ffn_quantum_weights_imag': 59.596}
    for name, (base, spread) in spreads.items():
        noise = np.random.default_rng([zlib.crc32(name.encode()), seed]).standard_normal(out[name].shape)
        drawn = base * np.exp(spread * noise) if base else spread * noise
        out[name] = jnp.asarray(drawn.astype(out[name].dtype))
    for name, factor in factors.items():
        out[name] = (out[name] * factor).astype(out[name].dtype)
    return out
```

```python
from contextlib import ExitStack

import numpy as np

import concourse.bass as bass
from concourse import mybir

F32 = mybir.dt.float32
BF16 = mybir.dt.bfloat16
ALU = mybir.AluOpType
ACT = mybir.ActivationFunctionType
AX = mybir.AxisListType.X

P = 128
B, S, D = 4, 1024, 128
H, HD, KV = 16, 8, 4
T = B * S // P
GT = 4
NG = T // GT
GW = GT * P
E, F0 = 8, 352
FCH = [(0, 128), (128, 128), (256, 96)]
F1 = 512
FC = F1 // P
LN_EPS = 1e-5
RMS_EPS = float(np.finfo(np.float32).eps)
SCALE = 1.0 / float(np.sqrt(D))
MASKED = -1e30

NQ = B * 4
SPL = 3
CROSS = SPL * SPL * HD
KROWS = CROSS + SPL
SLOTS = 4
PR = 8
HALF = 512

TWO_PI = 2.0 * np.pi
C1 = 6.28125
C2 = float(TWO_PI - C1)
ROUND = 12582912.0
PI_IN = 3.1415925


AT_ONE = 1


class Chain:

    def __init__(self, eng, sem, own_wait=False):
        self.eng, self.sem, self.start, self.n, self.own_wait = eng, sem, 0, 0, own_wait

    def done(self, ins):
        self.n += 1
        ins.then_inc(self.sem, 1)
        self.eng.wait_ge(self.sem, self.start + self.n)
        if self.own_wait:
            self.eng.nop(nofuse=True)

    def loop(self, turn, each):
        self.first = self.start + self.n
        self.start, self.n = self.first + turn * each, 0

    def end_loop(self, turns, each):
        assert self.n == each, (self.n, each)
        self.start, self.n = self.first + turns * each, 0


class Heads:

    def __init__(self, causal, letters):
        self.causal = causal
        self.groups = [(h, t) for h in range(2) for t in range(8) if not causal or t // 4 <= h]
        self.G = len(self.groups)
        self.last_of_half = [max(m for m, (h, _) in enumerate(self.groups) if h == half) for half in range(2)]
        self.events = self.order(letters)

    def cols(self, m):
        h, t = self.groups[m]
        return max(0, P * t - HALF * h) if self.causal else 0

    def diagonal(self, m):
        h, t = self.groups[m]
        return self.causal and t // 4 == h

    def keys(self, i):
        return P * (i + 1) if self.causal else S

    def order(self, letters):
        out, count = [], dict.fromkeys("abpmsctn", 0)
        for letter in letters:
            n = count[letter]
            count[letter] += 1
            if letter == "b":
                out.append(("B", n // 4, n % 4))
            elif letter == "a":
                out.append(("A", n))
            elif letter == "p":
                out.append(("PV", n))
            elif letter == "m":
                out.append(("MT", count["n"]))
            elif letter == "s":
                out.append(("MC",))
            elif letter == "t":
                out.append(("OT", n, count["s"]))
            else:
                out.append(({"c": "OC", "n": "ON"}[letter], n))
        assert list(count.values()) == [32, 4 * self.G, self.G, 1, 1, 2, 2, 2]
        return out


ORDERS = [
    "bbabbabababpbbaabbpbbaabbpbbbapbacabbatbababpbbnaabbpbabpababababababpbababpbabpbabmsababbabbppaactn",
    "bbbbabbpbbaabbpbbaabbpbbaabbpbbaabbpbbaabbpbbaabbpbbaabbpcbabtbabanbpbbpbbaabbpbbaabbpbababbpbbaabbpbbabmasbbapbbapcaatn",
]
LAYERS = [Heads(True, ORDERS[0]), Heads(False, ORDERS[1])]
QUAD_LOADS = 2 * SPL * SPL + 1


def build(nc, h_in, Wqvk, Wo0, router_w, gate_proj, up_proj, down_proj, w_q, w_k, w_v, w_o, g_rms,
          W1, b1, phases, w_real, w_imag, W2, b2, rope, out):
    q_parts = [nc.dram_tensor(f"q_parts{l}", (SPL, P, B * S), BF16, kind="Internal").ap() for l in range(2)]
    k_parts = [nc.dram_tensor(f"k_parts{l}", (SPL, r, B * S), BF16, kind="Internal").ap()
               for l, r in enumerate((P, KV * HD))]
    x_dram = h_in.rearrange("b (t p) d -> p (b t) d", p=P)
    out_dram = out.rearrange("b (t p) d -> p (b t) d", p=P)

    with ExitStack() as ctx:
        def sb(name, shape, dt=F32):
            return ctx.enter_context(nc.sbuf_tensor(name, shape, dt))

        def sem(name):
            return ctx.enter_context(nc.semaphore(name))

        x = sb("x", [P, T, D])
        attn = sb("attn", [P, T, D])
        v1 = sb("v1", [P, T, H * (HD + 1)])
        Q = sb("Q", [P, SLOTS, 4, S], BF16)
        K = sb("K", [P, SLOTS, 4, S], BF16)
        V = sb("V", [P, SLOTS, 8, 4 * (HD + 1)])
        probs = sb("probs", [P, PR, HALF])
        oT = sb("oT", [P, HALF])
        rowmax = sb("rowmax", [P, 2, 32])
        negmax = sb("negmax", [P, SPL, 32], BF16)
        negrest = sb("negrest", [P, 32])
        negmaxT = sb("negmaxT", [SPL * 32, P], BF16)
        rden = sb("rden", [P, 4, 4])
        spare = Q[:, :, :, :].rearrange("p s j n -> p (s j n)").bitcast(F32)
        hT_all = spare[:, 0:B * S]
        acts = spare[:, B * S:B * S + 6 * GW].rearrange("p (a c n) -> p a c n", a=2, c=len(FCH))
        gated = spare[:, B * S + 6 * GW:B * S + 8 * GW].rearrange("p (a n) -> p a n", a=2)
        act1 = spare[:, B * S:B * S + FC * GW].rearrange("p (c n) -> p c n", c=FC)
        ident = sb("ident", [P, P])
        identb = sb("identb", [P, P], BF16)
        causal = sb("causal", [P, P], BF16)
        wqvk = sb("wqvk", [P, 3 * D])
        wo0 = sb("wo0", [P, D])
        wr = sb("wr", [P, E])
        wg = sb("wg", [P, E, F0])
        wu = sb("wu", [P, E, F0])
        wd = sb("wd", [P, len(FCH), E, D])
        wq1 = sb("wq1", [P, D])
        wk1 = sb("wk1", [P, KV * HD])
        wv1 = sb("wv1", [P, KV * HD])
        wo1 = sb("wo1", [P, D])
        gcol = sb("gcol", [P, 1])
        w1 = sb("w1", [P, F1])
        w2 = sb("w2", [P, FC, D])
        b1c = sb("b1c", [P, FC])
        th = sb("th", [P, FC])
        wrl = sb("wrl", [P, FC])
        wim = sb("wim", [P, FC])
        b2r = sb("b2r", [P, D])
        ropeT = sb("ropeT", [P, S])
        stats = sb("stats", [P, GT, 6])
        mv = sb("mv", [P, GT, 2])
        rstd = sb("rstd", [P, GT])
        rtmp = sb("rtmp", [P, GT])
        rms = sb("rms", [P, GT])
        power = sb("power", [P, GT])
        tokens = sb("tokens", [P, GT, D])
        tokens2 = sb("tokens2", [P, GT, D])
        hT = sb("hT", [P, GW])
        aT = sb("aT", [P, GW])
        qk32 = probs[:, 0:2, :]
        rest = probs[:, 2:4, :]
        parts = probs[:, 4:7, :].rearrange("p a n -> p (a n)").bitcast(BF16)\
            .rearrange("p (a c n) -> p a c n", a=2, c=SPL)
        ew = sb("ew", [P, T, E])
        lower = sb("lower", [P, E, E])
        ra = sb("ra", [P, GT, E])
        rb = sb("rb", [P, GT, E])
        rc = sb("rc", [P, GT, E])
        r1 = sb("r1", [P, GT])
        r2 = sb("r2", [P, GT])
        cmp1 = sb("cmp1", [P, GT, E, E])
        cmp2 = sb("cmp2", [P, GT, E, E])
        tc1 = sb("tc1", [P, FC])
        tc2 = sb("tc2", [P, FC])
        thr = sb("thr", [P, FC])
        thc = sb("thc", [P, FC])
        sin_th = sb("sin_th", [P, FC])
        cos_th = sb("cos_th", [P, FC])
        coef = sb("coef", [P, FC])
        hid = probs[:, 0:2, :]
        arg = probs[:, 2:4, :]
        turns = probs[:, 4:6, :]
        sine = probs[:, 6:8, :]
        y = sb("y", [P, GT, D])

        ps = ctx.enter_context(nc.psum_tensor("ps", [P, 8, 512], F32))
        def score_a(n):
            return ps[:, 2 * n:2 * n + 2, :].rearrange("p b n -> p (b n)")

        PV_BANK, MISC = 6, 7

        x_in, w_in = sem("x_in"), sem("w_in")
        consts = sem("consts")
        vec, pool_own, act_own = sem("vector_own"), sem("gpsimd_own"), sem("scalar_own")
        names = ("normed", "turned", "h_ready", "stats_ready", "rstd_ready", "q_out", "k_out", "v_out", "qk_sb",
                 "v_taken", "split_done", "parts_written", "scores", "max_done", "negmax_ready", "negmaxT_psum",
                 "negmaxT_ready", "negmax_rows", "scoresT", "exp_done", "pv_done", "o_copied", "o_turned",
                 "attn_done")
        from_one = ("h_ready", "v_out", "qk_sb", "v_taken", "split_done", "parts_written", "o_copied", "o_turned",
                    "attn_done")
        s = [{n: sem(f"{n}{l}") for n in names} for l in range(2)]
        loaded = [[sem(f"loaded{l}_{k}") for k in range(SLOTS)] for l in range(2)]
        pre = {n: sem("pre_" + n) for n in
               ("attn_staged", "a_turned", "a_ready", "wo_out", "stats", "rstd", "normed", "turned", "h_ready",
                "logits", "shifted", "exped", "weights")}
        moe = {n: sem("moe_" + n) for n in ("gate", "up", "silu", "mul", "down", "acc")}
        ff = {n: sem("ff_" + n) for n in
              ("attn_staged", "a_turned", "a_ready", "wo_out", "added", "stats", "rstd", "normed", "turned", "h_ready",
               "hidden", "arg", "turns", "reduced", "clamped", "sine", "mixed", "relu", "y_out", "y_ready", "stored")}
        theta = {n: sem("theta_" + n) for n in ("reduced", "sines", "coef")}

        weights = [
            (wqvk[:, :], Wqvk), (wo0[:, :], Wo0), (wr[:, :], router_w),
            (wg[:, :, :], gate_proj.rearrange("e d f -> d e f")), (wu[:, :, :], up_proj.rearrange("e d f -> d e f")),
            *[(wd[0:w, c, :, :], down_proj[:, f:f + w, :].rearrange("e f d -> f e d")) for c, (f, w) in enumerate(FCH)],
            (wq1[:, :], w_q), (wk1[:, :], w_k), (wv1[:, :], w_v), (wo1[:, :], w_o), (gcol[:, :], g_rms),
            (w1[:, :], W1), (w2[:, :, :], W2.rearrange("(c p) d -> p c d", p=P)), (b1c[:, :], b1),
            (th[:, :], phases), (wrl[:, :], w_real), (wim[:, :], w_imag),
            (b2r[:, :], b2.rearrange("(a d) -> a d", a=1).broadcast_to([P, D])), (ropeT[:, :], rope),
        ]

        starting = [s[l][n] for l in range(2) for n in from_one] + [moe["down"]] + \
            [ff[n] for n in ("h_ready", "arg", "y_ready", "a_turned", "y_out", "stored")]

        block = ctx.enter_context(nc.Block())

        def apart(eng):
            eng.nop(nofuse=True)

        @block.sync
        def _(sp):
            sp.dma_start(x[:, :, :], x_dram).then_inc(x_in, 16)
            for semaphore in starting:
                sp.sem_inc(semaphore, 1)
            for l in range(2):
                sl = s[l]
                rows_k = P if l == 0 else KV * HD

                with sp.Fori(0, NG) as u:
                    sp.wait_ge(sl["split_done"], 2 * u + 2 + AT_ONE)
                    sp.dma_start(q_parts[l][:, :, bass.ts(u, GW)].rearrange("c p n -> p c n"),
                                 parts[:, 0, :, :]).then_inc(sl["parts_written"], 16)
                    sp.dma_start(k_parts[l][:, :, bass.ts(u, GW)].rearrange("c p n -> p c n"),
                                 parts[0:rows_k, 1, :, :]).then_inc(sl["parts_written"], 16)
                sp.wait_ge(sl["parts_written"], 32 * NG + AT_ONE)

                def load(b, q):
                    for a in range(SPL):
                        heads = q_parts[l][a, :, bass.ts(b, S)].rearrange("(h i) n -> i h n", i=HD)
                        heads = heads[:, 4 * q:4 * q + 4, :] if l == 0 else heads[:, q:H:KV, :]
                        for r in range(SPL):
                            row = (a * SPL + r) * HD
                            sp.dma_start(Q[row:row + HD, q, :, :], heads).then_inc(loaded[l][q], 16)
                            keys = k_parts[l][r, :, bass.ts(b, S)].rearrange("(h i) n -> i h n", i=HD)
                            keys = keys[:, 4 * q:4 * q + 4, :] if l == 0 else keys[:, q:q + 1, :]
                            sp.dma_start(K[row:row + HD, q, 0:keys.shape[1], :], keys).then_inc(loaded[l][q], 16)
                    w = (HD + 1) * (4 if l == 0 else 1)
                    sp.dma_start(V[:, q, :, 0:w], v1[:, bass.ts(b, 8), w * q:w * q + w]).then_inc(loaded[l][q], 16)

                def negmax_rows(q, g):
                    sp.wait_ge(sl["negmaxT_ready"], g + 1)
                    for c in range(SPL):
                        sp.dma_start(Q[CROSS + c:CROSS + c + 1, q, :, :].rearrange("c j (i n) -> c (j i) n", n=P),
                                     negmaxT[32 * c:32 * c + 32, :]).then_inc(sl["negmax_rows"], 16)

                sp.wait_ge(consts, 6)
                sp.wait_ge(sl["v_taken"], NG + AT_ONE)
                for q in range(3):
                    load(0, q)
                negmax_rows(0, 0)

                def batch(b, final):
                    for q in range(4):
                        g = 4 * b + q
                        if q == 0 or not final:
                            sp.wait_ge(sl["o_turned"], 2 * g + AT_ONE)
                            load(b if q == 0 else b + 1, (q + 3) % 4)
                        if q < 3 or not final:
                            negmax_rows((q + 1) % 4, g + 1)

                with sp.Fori(0, B - 1) as b:
                    batch(b, False)
                batch(B - 1, True)

            with sp.Fori(0, NG) as u:
                sp.wait_ge(ff["y_ready"], u + 1 + AT_ONE)
                sp.dma_start(out_dram[:, bass.ts(u, GT), :], y[:, :, :]).then_inc(ff["stored"], 16)
            sp.wait_ge(ff["stored"], 16 * NG + AT_ONE)

        @block.gpsimd
        def _(pool):
            own = Chain(pool, pool_own, own_wait=True)
            own.done(pool.memset(ident[:, :], 0.0))
            own.done(pool.memset(identb[:, :], 0.0))
            own.done(pool.memset(causal[:, :], 0.0))
            own.done(pool.memset(lower[:, :, :], 0.0))
            own.done(pool.memset(power[:, :], -0.5))
            for m in (ident, identb):
                pool.affine_select(out=m[:, :], in_=m[:, :], compare_op=ALU.not_equal, fill=1.0, base=0,
                                   pattern=[[-1, P]], channel_multiplier=1).then_inc(consts, 1)
            pool.affine_select(out=causal[:, :], in_=causal[:, :], compare_op=ALU.is_ge, fill=MASKED, base=0,
                               pattern=[[-1, P]], channel_multiplier=1).then_inc(consts, 1)
            pool.affine_select(out=lower[:, :, :], in_=lower[:, :, :], compare_op=ALU.is_ge, fill=1.0, base=0,
                               pattern=[[-1, E], [1, E]], channel_multiplier=0).then_inc(consts, 1)
            own.done(pool.memset(v1[:, :, :], 1.0))
            pool.memset(K[64:96, :, :, :], 1.0).then_inc(consts, 1)

            def inverse(ready, done, u, with_rms=False):
                pool.wait_ge(ready, u + 1)
                apart(pool)
                if not with_rms:
                    own.done(pool.tensor_scalar(rtmp[:, :], mv[:, :, 1], LN_EPS, 1.0, ALU.add, ALU.mult))
                    pool.tensor_tensor(rstd[:, :], rtmp[:, :], power[:, :], ALU.pow).then_inc(done, 1)
                    return
                own.done(pool.tensor_scalar(rtmp[:, :], mv[:, :, 1], LN_EPS, 1.0, ALU.add, ALU.mult))
                own.done(pool.tensor_tensor(rms[:, :], rtmp[:, :], power[:, :], ALU.pow))
                own.done(pool.tensor_tensor(rtmp[:, :], mv[:, :, 1], rms[:, :], ALU.mult))
                own.done(pool.tensor_tensor(rtmp[:, :], rtmp[:, :], rms[:, :], ALU.mult))
                own.done(pool.tensor_scalar(rtmp[:, :], rtmp[:, :], RMS_EPS, 1.0, ALU.add, ALU.mult))
                own.done(pool.tensor_tensor(rtmp[:, :], rtmp[:, :], power[:, :], ALU.pow))
                pool.tensor_tensor(rstd[:, :], rms[:, :], rtmp[:, :], ALU.mult).then_inc(done, 1)

            with pool.Fori(0, NG) as u:
                own.loop(u, 1)
                inverse(s[0]["stats_ready"], s[0]["rstd_ready"], u)
            own.end_loop(NG, 1)
            with pool.Fori(0, NG) as u:
                own.loop(u, 1)
                inverse(pre["stats"], pre["rstd"], u)
            own.end_loop(NG, 1)
            with pool.Fori(0, NG) as u:
                own.loop(u, 6)
                inverse(s[1]["stats_ready"], s[1]["rstd_ready"], u, True)
            own.end_loop(NG, 6)

            def turn_counts(u, c):
                n = FC * u + c
                pool.wait_ge(ff["arg"], n + 1 + AT_ONE)
                apart(pool)
                own.done(pool.tensor_scalar(turns[:, c % 2, :], arg[:, c % 2, :], 1.0 / TWO_PI, ROUND,
                                            ALU.mult, ALU.add))
                pool.tensor_scalar(turns[:, c % 2, :], turns[:, c % 2, :], -ROUND, 1.0,
                                   ALU.add, ALU.mult).then_inc(ff["turns"], 1)

            def clamp(u, c):
                n = FC * u + c
                pool.wait_ge(ff["reduced"], n + 1)
                apart(pool)
                pool.tensor_scalar(arg[:, c % 2, :], arg[:, c % 2, :], PI_IN, -PI_IN,
                                   ALU.min, ALU.max).then_inc(ff["clamped"], 1)

            with pool.Fori(0, NG) as u:
                own.loop(u, FC + 1)
                inverse(ff["stats"], ff["rstd"], u)
                for c in range(FC):
                    turn_counts(u, c)
                    if c:
                        clamp(u, c - 1)
                clamp(u, FC - 1)
            own.end_loop(NG, FC + 1)

        @block.tensor
        def _(pe):
            def turn(src, bank, done):
                for k in range(GT):
                    last = pe.transpose(ps[:, bank, k * P:(k + 1) * P], src[:, k, :], ident[:, :])
                last.then_inc(done, 1)

            def project(l):
                sl = s[l]
                with pe.Fori(0, NG) as u:
                    pe.wait_ge(sl["normed"], u + 1)
                    pe.wait_ge(sl["h_ready"], u + AT_ONE)
                    turn(tokens, 0, sl["turned"])
                    pe.wait_ge(sl["h_ready"], u + 1 + AT_ONE)
                    pe.wait_ge(sl["qk_sb"], 2 * u + AT_ONE)
                    pe.wait_ge(sl["v_taken"], u + AT_ONE)
                    if l == 0:
                        wq, wv, wk = (wqvk[:, n * D:(n + 1) * D] for n in range(3))
                        rk, wd_v = P, D
                    else:
                        wq, wk, wv, rk, wd_v = wq1[:, :], wk1[:, :], wv1[:, :], KV * HD, KV * HD
                    pe.matmul(ps[:, 1, :], wq, hT[:, :], start=True, stop=True).then_inc(sl["q_out"], 1)
                    pe.matmul(ps[0:rk, 2, :], wk, hT[:, :], start=True, stop=True).then_inc(sl["k_out"], 1)
                    for k in range(GT):
                        last = pe.matmul(ps[:, 3, k * wd_v:(k + 1) * wd_v], hT[:, k * P:(k + 1) * P], wv,
                                         start=True, stop=True)
                    last.then_inc(sl["v_out"], 1)

            def attention(l):
                sl, hd = s[l], LAYERS[l]
                G, nB = hd.G, 4 * hd.G
                rows = HD + 1

                def pass_a(quad, slot, j, i):
                    n = 32 * quad + 8 * j + i
                    buf = score_a(i % 2)
                    kj = j if l == 0 else 0
                    if not isinstance(n, int) or n >= 2:
                        pe.wait_ge(sl["max_done"], n - 1)
                    w = hd.keys(i)
                    for c in range(0, w, 512):
                        e = min(c + 512, w)
                        diag = hd.causal and e == w
                        last = pe.matmul(buf[:, c:e], Q[0:CROSS, slot, j, i * P:(i + 1) * P],
                                         K[0:CROSS, slot, kj, c:e], start=True, stop=not diag)
                        if diag:
                            last = pe.matmul(buf[:, w - P:w], identb[:, :], causal[:, :],
                                             start=False, stop=True)
                    last.then_inc(sl["scores"], 1)

                def pass_b(g, q, m, j):
                    n = nB * g + 4 * m + j
                    h, t = hd.groups[m]
                    c = hd.cols(m)
                    pe.wait_ge(sl["exp_done"], n + 1)
                    kj = j if l == 0 else 0
                    diag = hd.diagonal(m)
                    last = pe.matmul(ps[:, 4 + j % 2, c:HALF], K[0:KROWS, q, kj, t * P:(t + 1) * P],
                                     Q[0:KROWS, q, j, h * HALF + c:(h + 1) * HALF], start=True, stop=not diag)
                    if diag:
                        last = pe.matmul(ps[:, 4 + j % 2, c:c + P], causal[:, :], identb[:, :],
                                         start=False, stop=True)
                    last.then_inc(sl["scoresT"], 1)

                def pv(g, q, m):
                    h, t = hd.groups[m]
                    c = hd.cols(m)
                    if t == 0:
                        pe.wait_ge(sl["o_copied"], 2 * g + h + AT_ONE)
                    for j in range(4):
                        n = nB * g + 4 * m + j
                        pe.wait_ge(sl["exp_done"], n + 3)
                        kj = j if l == 0 else 0
                        last = pe.matmul(ps[32 * j:32 * j + rows, PV_BANK, c:HALF],
                                         V[:, q, t, kj * rows:(kj + 1) * rows],
                                         probs[:, (4 * m + j) % PR, c:HALF],
                                         start=(t == 0), stop=(m == hd.last_of_half[h]), skip_group_check=True)
                    last.then_inc(sl["pv_done"], 1)

                def negmax_turn(g, g_prev_norms):
                    pe.wait_ge(sl["negmax_ready"], g + 1)
                    pe.wait_ge(sl["attn_done"], g_prev_norms + AT_ONE)
                    pe.transpose(ps[0:SPL * 32, MISC, 0:P // 2].bitcast(BF16),
                                 negmax[:, :, :].rearrange("p c n -> p (c n)"), identb[:, :])\
                        .then_inc(sl["negmaxT_psum"], 1)

                def out_turn(g, h, turned_max):
                    pe.wait_ge(sl["o_copied"], 2 * g + h + 1 + AT_ONE)
                    pe.wait_ge(sl["attn_done"], 2 * g + h + AT_ONE)
                    pe.wait_ge(sl["negmaxT_ready"], turned_max)
                    for k in range(4):
                        last = pe.transpose(ps[:, MISC, k * P:(k + 1) * P], oT[:, k * P:(k + 1) * P], ident[:, :])
                    last.then_inc(sl["o_turned"], 1)

                def quad_loaded(b, q):
                    pe.wait_ge(loaded[l][q], 16 * QUAD_LOADS * (b + 1))

                quad_loaded(0, 0)
                for n in range(32):
                    pass_a(0, 0, n // 8, n % 8)
                quad_loaded(0, 1)
                for n in range(8):
                    pass_a(1, 1, 0, n)
                negmax_turn(0, 0)

                def batch(b, final):
                    for q in range(4):
                        g = 4 * b + q
                        more_1, more_2 = not (final and q == 3), not (final and q >= 2)
                        pe.wait_ge(sl["negmax_rows"], 16 * SPL * (g + 1))
                        for ev in hd.events:
                            if ev[0] == "B":
                                pass_b(g, q, ev[1], ev[2])
                            elif ev[0] == "A":
                                k = ev[1]
                                if k < 24 and more_1:
                                    pass_a(g + 1, (q + 1) % 4, 1 + k // 8, k % 8)
                                if k >= 24 and more_2:
                                    if k == 24:
                                        quad_loaded(b + (q >= 2), (q + 2) % 4)
                                    pass_a(g + 2, (q + 2) % 4, 0, k % 8)
                            elif ev[0] == "PV":
                                pv(g, q, ev[1])
                            elif ev[0] == "MT" and more_1:
                                negmax_turn(g + 1, 2 * g + ev[1])
                            elif ev[0] == "OT":
                                out_turn(g, ev[1], g + 1 + (ev[2] if more_1 else 0))

                with pe.Fori(0, B - 1) as b:
                    batch(b, False)
                batch(B - 1, True)

            def prepare(u, stage):
                if stage == 0:
                    pe.wait_ge(pre["attn_staged"], u + 1)
                    pe.wait_ge(pre["h_ready"], u)
                    turn(tokens, 6, pre["a_turned"])
                elif stage == 1:
                    pe.wait_ge(pre["a_ready"], u + 1)
                    pe.wait_ge(pre["weights"], u)
                    for k in range(GT):
                        last = pe.matmul(ps[:, 7, k * D:(k + 1) * D], aT[:, k * P:(k + 1) * P], wo0[:, :],
                                         start=True, stop=True)
                    last.then_inc(pre["wo_out"], 1)
                elif stage == 2:
                    pe.wait_ge(pre["normed"], u + 1)
                    turn(tokens2, 6, pre["turned"])
                else:
                    pe.wait_ge(pre["h_ready"], u + 1)
                    for k in range(GT):
                        last = pe.matmul(ps[:, 7, k * E:(k + 1) * E], hT[:, k * P:(k + 1) * P], wr[:, :],
                                         start=True, stop=True)
                    last.then_inc(pre["logits"], 1)

            def gate_up(u, e):
                for c, (f, w) in enumerate(FCH):
                    n = 3 * (E * u + e) + c
                    par = (3 * e + c) % 2
                    moving = hT_all[:, bass.ts(u, GW)]
                    pe.wait_ge(moe["silu"], n + 1)
                    pe.matmul(ps[0:w, par, :], wg[:, e, f:f + w], moving,
                              start=True, stop=True).then_inc(moe["gate"], 1)
                    pe.wait_ge(moe["mul"], n + 1)
                    pe.matmul(ps[0:w, 2 + par, :], wu[:, e, f:f + w], moving,
                              start=True, stop=True).then_inc(moe["up"], 1)

            def down(u, e):
                n = E * u + e
                pe.wait_ge(moe["mul"], 3 * n + 5)
                pe.wait_ge(moe["acc"], n + 1)
                for k in range(GT):
                    for c, (f, w) in enumerate(FCH):
                        last = pe.matmul(ps[:, 4 + e % 2, k * D:(k + 1) * D],
                                         acts[0:w, e % 2, c, k * P:(k + 1) * P], wd[0:w, c, e, :],
                                         start=(c == 0), stop=(c == len(FCH) - 1))
                last.then_inc(moe["down"], 1)

            def experts(u, more):
                for e in range(E):
                    gate_up(u, e)
                    if e:
                        down(u, e - 1)
                    if more and e % 2:
                        prepare(u + 1, e // 2)
                down(u, E - 1)

            def ff_prepare(u):
                pe.wait_ge(ff["attn_staged"], u + 1)
                pe.wait_ge(ff["h_ready"], u + AT_ONE)
                turn(tokens, 0, ff["a_turned"])
                pe.wait_ge(ff["a_ready"], u + 1)
                for k in range(GT):
                    last = pe.matmul(ps[:, 1, k * D:(k + 1) * D], aT[:, k * P:(k + 1) * P], wo1[:, :],
                                     start=True, stop=True)
                last.then_inc(ff["wo_out"], 1)
                pe.wait_ge(ff["normed"], u + 1)
                turn(tokens2, 0, ff["turned"])

            def ff_out(u):
                pe.wait_ge(ff["relu"], FC * u + FC)
                pe.wait_ge(ff["y_ready"], u + AT_ONE)
                for k in range(GT):
                    for c in range(FC):
                        last = pe.matmul(ps[:, 6, k * D:(k + 1) * D], act1[:, c, k * P:(k + 1) * P], w2[:, c, :],
                                         start=(c == 0), stop=(c == FC - 1))
                last.then_inc(ff["y_out"], 1)

            pe.wait_ge(consts, 6)
            pe.wait_ge(w_in, 16 * len(weights))
            project(0)
            attention(0)
            for stage in range(4):
                prepare(0, stage)
            with pe.Fori(0, NG - 1) as u:
                experts(u, True)
            experts(NG - 1, False)
            project(1)
            attention(1)
            with pe.Fori(0, NG) as u:
                ff_prepare(u)
                pe.wait_ge(ff["h_ready"], u + 1 + AT_ONE)
                for c in range(FC):
                    pe.wait_ge(ff["arg"], FC * u + AT_ONE)
                    pe.matmul(ps[:, 2 + c, :], w1[:, c * P:(c + 1) * P], hT[:, :],
                              start=True, stop=True).then_inc(ff["hidden"], 1)
                ff_out(u)

        @block.scalar
        def _(act):
            own = Chain(act, act_own)
            for dst, src in weights:
                act.dma_start(dst, src).then_inc(w_in, 16)
            act.sem_inc(moe["silu"], 2)
            for l in range(2):
                act.sem_inc(s[l]["exp_done"], 2)
            act.wait_ge(consts, 6)
            act.wait_ge(w_in, 16 * len(weights))

            act.wait_ge(theta["reduced"], 1)
            act.activation(sin_th[:, :], thr[:, :], ACT.Sin).then_inc(theta["sines"], 1)
            act.activation(cos_th[:, :], thc[:, :], ACT.Sin).then_inc(theta["sines"], 1)

            def project(l):
                sl = s[l]
                with act.Fori(0, NG) as u:
                    act.wait_ge(sl["turned"], u + 1)
                    act.wait_ge(sl["v_out"], u + AT_ONE)
                    if l == 0:
                        act.activation(hT[:, :], ps[:, 0, :], ACT.Copy).then_inc(sl["h_ready"], 1)
                    else:
                        act.activation(hT[:, :], ps[:, 0, :], ACT.Copy, scale=gcol[:, 0:1])\
                            .then_inc(sl["h_ready"], 1)
                    if l == 0:
                        act.wait_ge(sl["split_done"], 2 * u + AT_ONE)
                        act.wait_ge(sl["q_out"], u + 1)
                        act.activation(qk32[:, 0, :], ps[:, 1, :], ACT.Copy).then_inc(sl["qk_sb"], 1)
                        act.wait_ge(sl["k_out"], u + 1)
                        act.activation(qk32[:, 1, :], ps[:, 2, :], ACT.Copy).then_inc(sl["qk_sb"], 1)
                    nh = H if l == 0 else KV
                    act.wait_ge(sl["v_out"], u + 1 + AT_ONE)
                    act.activation(v1[:, bass.ts(u, GT), 0:nh * (HD + 1)]
                                   .rearrange("p t (h i) -> p t h i", i=HD + 1)[:, :, :, 0:HD],
                                   ps[:, 3, 0:GT * nh * HD].rearrange("p (t h i) -> p t h i", t=GT, i=HD),
                                   ACT.Copy).then_inc(sl["v_taken"], 1)

            def attention(l):
                sl, hd = s[l], LAYERS[l]
                G, nB = hd.G, 4 * hd.G

                def negmax_copy(g):
                    act.wait_ge(sl["negmaxT_psum"], g + 1)
                    if not isinstance(g, int) or g > 0:
                        act.wait_ge(sl["negmax_rows"], 16 * SPL * g)
                    act.activation(negmaxT[:, :], ps[0:SPL * 32, MISC, 0:P // 2].bitcast(BF16),
                                   ACT.Copy).then_inc(sl["negmaxT_ready"], 1)

                negmax_copy(0)

                def batch(b, final):
                    for q in range(4):
                        g = 4 * b + q
                        for ev in hd.events:
                            if ev[0] == "B":
                                m, j = ev[1], ev[2]
                                n = nB * g + 4 * m + j
                                c = hd.cols(m)
                                act.wait_ge(sl["scoresT"], n + 1)
                                if j == 0:
                                    act.wait_ge(sl["pv_done"], G * g + m + 1)
                                act.activation(probs[:, (4 * m + j) % PR, c:HALF], ps[:, 4 + j % 2, c:HALF],
                                               ACT.Exp, scale=SCALE).then_inc(sl["exp_done"], 1)
                            elif ev[0] == "OC":
                                act.wait_ge(sl["pv_done"], G * g + hd.last_of_half[ev[1]] + 3)
                                act.activation(oT[:, :], ps[:, PV_BANK, :], ACT.Copy)\
                                    .then_inc(sl["o_copied"], 1)
                            elif ev[0] == "MC" and not (final and q == 3):
                                negmax_copy(g + 1)

                with act.Fori(0, B - 1) as b:
                    batch(b, False)
                batch(B - 1, True)

            def prepare(u, stage):
                if stage == 0:
                    act.wait_ge(pre["a_turned"], u + 1)
                    act.activation(aT[:, :], ps[:, 6, :], ACT.Copy).then_inc(pre["a_ready"], 1)
                elif stage == 2:
                    act.wait_ge(pre["turned"], u + 1)
                    act.wait_ge(pre["logits"], u)
                    act.activation(hT[:, :], ps[:, 6, :], ACT.Copy)
                    act.activation(hT_all[:, bass.ts(u, GW)], ps[:, 6, :], ACT.Copy).then_inc(pre["h_ready"], 1)
                elif stage == 3:
                    act.wait_ge(pre["shifted"], u + 1)
                    act.activation(rb[:, :, :], ra[:, :, :], ACT.Exp).then_inc(pre["exped"], 1)

            def experts(u, more):
                for e in range(E):
                    for c, (f, w) in enumerate(FCH):
                        n = 3 * (E * u + e) + c
                        par = (3 * e + c) % 2
                        act.wait_ge(moe["gate"], n + 1)
                        act.wait_ge(moe["mul"], n + 1)
                        act.activation(gated[0:w, par, :], ps[0:w, par, :], ACT.Silu).then_inc(moe["silu"], 1)
                    if more and e in (1, 5, 7):
                        prepare(u + 1, e // 2)

            project(0)
            attention(0)
            for stage in range(4):
                prepare(0, stage)
            with act.Fori(0, NG - 1) as u:
                experts(u, True)
            experts(NG - 1, False)
            project(1)
            attention(1)
            with act.Fori(0, NG) as u:
                own.loop(u, FC)
                act.wait_ge(ff["a_turned"], u + 1 + AT_ONE)
                act.activation(aT[:, :], ps[:, 0, :], ACT.Copy).then_inc(ff["a_ready"], 1)
                act.wait_ge(ff["turned"], u + 1)
                act.activation(hT[:, :], ps[:, 0, :], ACT.Copy).then_inc(ff["h_ready"], 1)

                def hidden(c):
                    n = FC * u + c
                    act.wait_ge(ff["hidden"], n + 1)
                    if c >= 2:
                        act.wait_ge(ff["relu"], n - 1)
                    own.done(act.activation(hid[:, c % 2, :], ps[:, 2 + c, :], ACT.Identity, bias=b1c[:, c:c + 1]))
                    act.activation(arg[:, c % 2, :], hid[:, c % 2, :], ACT.Identity, bias=thr[:, c:c + 1],
                                   scale=0.1).then_inc(ff["arg"], 1)

                def sines(c):
                    n = FC * u + c
                    act.wait_ge(ff["clamped"], n + 1)
                    act.activation(sine[:, c % 2, :], arg[:, c % 2, :], ACT.Sin).then_inc(ff["sine"], 1)
                    act.wait_ge(ff["mixed"], n + 1)
                    if c == 0:
                        act.wait_ge(ff["y_out"], u + AT_ONE)
                    act.activation(act1[:, c, :], sine[:, c % 2, :], ACT.Relu).then_inc(ff["relu"], 1)

                for c in range(FC):
                    hidden(c)
                    if c:
                        sines(c - 1)
                sines(FC - 1)
            own.end_loop(NG, FC)

        @block.vector
        def _(dve):
            own = Chain(dve, vec)
            dve.sem_inc(moe["mul"], 2)
            dve.memset(ps[:, PV_BANK, :], 0.0).then_inc(consts, 1)
            dve.sem_inc(moe["acc"], 2)
            for l in range(2):
                dve.sem_inc(s[l]["pv_done"], 2)

            def reduce_angle(dst, src):
                own.done(dve.tensor_scalar(tc1[:, :], src, 1.0 / TWO_PI, ROUND, ALU.mult, ALU.add))
                own.done(dve.tensor_scalar(tc1[:, :], tc1[:, :], ROUND, None, ALU.subtract))
                own.done(dve.scalar_tensor_tensor(tc2[:, :], tc1[:, :], -C1, src, ALU.mult, ALU.add))
                own.done(dve.scalar_tensor_tensor(tc2[:, :], tc1[:, :], -C2, tc2[:, :], ALU.mult, ALU.add))
                own.done(dve.tensor_scalar(dst, tc2[:, :], PI_IN, -PI_IN, ALU.min, ALU.max))

            dve.wait_ge(w_in, 16 * len(weights))
            reduce_angle(thr[:, :], th[:, :])
            own.done(dve.tensor_scalar(thc[:, :], thr[:, :], float(np.pi / 2), None, ALU.add))
            reduce_angle(thc[:, :], thc[:, :])
            dve.tensor_copy(thc[:, :], thc[:, :]).then_inc(theta["reduced"], 1)
            dve.wait_ge(theta["sines"], 2)
            own.done(dve.tensor_tensor(cos_th[:, :], cos_th[:, :], wrl[:, :], ALU.mult))
            own.done(dve.tensor_tensor(sin_th[:, :], sin_th[:, :], wim[:, :], ALU.mult))
            own.done(dve.tensor_tensor(cos_th[:, :], cos_th[:, :], sin_th[:, :], ALU.add))
            own.done(dve.scalar_tensor_tensor(coef[:, :], cos_th[:, :], 0.1, wim[:, :], ALU.mult, ALU.mult))

            CH_STATS = 4

            def statistics(u, ready):
                apart(dve)
                for k in range(GT):
                    last = dve.bn_stats(stats[:, k, :], x[:, u * GT + k, :])
                own.done(last)
                apart(dve)
                for k in range(GT):
                    last = dve.bn_aggr(mv[:, k, :], stats[:, k, :])
                last.then_inc(ready, 1)

            def normalise(u, rstd_ready, dst, done):
                dve.wait_ge(rstd_ready, u + 1)
                for k in range(GT):
                    last = dve.tensor_scalar(dst[:, k, :], x[:, u * GT + k, :], mv[:, k, 0:1], rstd[:, k:k + 1],
                                             ALU.subtract, ALU.mult)
                last.then_inc(done, 1)

            def project(l):
                sl = s[l]

                def norm(u):
                    statistics(u, sl["stats_ready"])
                    dve.wait_ge(sl["stats_ready"], u + 1)
                    dve.wait_ge(sl["turned"], u)
                    normalise(u, sl["rstd_ready"], tokens, sl["normed"])

                def split(u, half):
                    rows = (P, P if l == 0 else KV * HD)
                    if l == 1:
                        for n, out_sem in enumerate(("q_out", "k_out")):
                            dve.wait_ge(sl[out_sem], u + 1)
                            r = rows[n]
                            dve.wait_ge(sl["split_done"], 2 * u + AT_ONE)
                            dve.tensor_tensor(qk32[0:r, n, :], ps[0:r, 1 + n, :], ropeT[0:r, half * GW:(half + 1) * GW], ALU.mult)\
                                .then_inc(sl["qk_sb"], 1)
                    dve.wait_ge(sl["parts_written"], 32 * u + AT_ONE)
                    for n in range(2):
                        r = rows[n]
                        dve.wait_ge(sl["qk_sb"], 2 * u + n + 1 + AT_ONE)
                        a, z, pt = qk32[0:r, n, :], rest[0:r, n, :], parts[0:r, n]
                        own.done(dve.tensor_copy(pt[:, 0, :], a))
                        own.done(dve.tensor_tensor(z, a, pt[:, 0, :], ALU.subtract))
                        own.done(dve.tensor_copy(pt[:, 1, :], z))
                        dve.tensor_tensor(pt[:, 2, :], z, pt[:, 1, :], ALU.subtract).then_inc(sl["split_done"], 1)

                norm(0)
                per = 2 * 7
                with dve.Fori(0, NG // 2 - 1) as v:
                    own.loop(v, per)
                    for half in range(2):
                        norm(2 * v + half + 1)
                        split(2 * v + half, half)
                own.end_loop(NG // 2 - 1, per)
                norm(NG - 1)
                split(NG - 2, 0)
                split(NG - 1, 1)

            def attention(l):
                sl, hd = s[l], LAYERS[l]

                def row_max(quad, j, i, par):
                    n = 32 * quad + 8 * j + i
                    dve.wait_ge(sl["scores"], n + 1)
                    dve.tensor_reduce(rowmax[:, par, 8 * j + i:8 * j + i + 1], score_a(i % 2)[:, 0:hd.keys(i)],
                                      AX, ALU.max).then_inc(sl["max_done"], 1)

                def negmax_split(g, par):
                    dve.wait_ge(sl["max_done"], 32 * g + 32)
                    if not isinstance(g, int) or g > 0:
                        dve.wait_ge(sl["negmaxT_psum"], g)
                    mx = rowmax[:, par, :]
                    own.done(dve.tensor_scalar(negmax[:, 0, :], mx, -1.0, None, ALU.mult))
                    own.done(dve.scalar_tensor_tensor(negrest[:, :], mx, -1.0, negmax[:, 0, :],
                                                      ALU.mult, ALU.subtract))
                    own.done(dve.tensor_copy(negmax[:, 1, :], negrest[:, :]))
                    dve.tensor_tensor(negmax[:, 2, :], negrest[:, :], negmax[:, 1, :], ALU.subtract)\
                        .then_inc(sl["negmax_ready"], 1)

                def normalise_out(g, b, q, h):
                    dve.wait_ge(sl["o_turned"], 2 * g + h + 1 + AT_ONE)
                    o = ps[:, MISC, :].rearrange("p (k j c) -> p k j c", k=4, c=32)
                    own.done(dve.reciprocal(rden[:, :, :], o[:, :, :, HD]))
                    dst = attn[:, bass.ds(8 * b + 4 * h, 4), :]
                    dst = dst.rearrange("p k (a c i) -> p k a c i", a=4, c=4)
                    dst = dst[:, :, q, :, :] if l == 0 else dst[:, :, :, q, :]
                    dve.tensor_tensor(dst, o[:, :, :, 0:HD], rden[:, :, :].unsqueeze(3).broadcast_to([P, 4, 4, HD]),
                                      ALU.mult).then_inc(sl["attn_done"], 1)

                for n in range(32):
                    row_max(0, n // 8, n % 8, 0)
                for n in range(8):
                    row_max(1, 0, n, 1)
                negmax_split(0, 0)

                def batch(b, final):
                    for q in range(4):
                        g = 4 * b + q
                        more_1, more_2 = not (final and q == 3), not (final and q >= 2)
                        for ev in hd.events:
                            if ev[0] == "A":
                                k = ev[1]
                                if k < 24 and more_1:
                                    row_max(g + 1, 1 + k // 8, k % 8, (q + 1) % 2)
                                if k >= 24 and more_2:
                                    row_max(g + 2, 0, k % 8, q % 2)
                                if k == 23 and more_1:
                                    negmax_split(g + 1, (q + 1) % 2)
                            elif ev[0] == "ON":
                                normalise_out(g, b, q, ev[1])

                per = 4 * (3 + 2)
                with dve.Fori(0, B - 1) as b:
                    own.loop(b, per)
                    batch(b, False)
                own.end_loop(B - 1, per)
                batch(B - 1, True)

            def prepare(u, stage):
                if stage == 0:
                    dve.tensor_copy(tokens[:, :, :], attn[:, bass.ts(u, GT), :]).then_inc(pre["attn_staged"], 1)
                elif stage == 1:
                    dve.wait_ge(pre["wo_out"], u + 1)
                    xs = x[:, bass.ts(u, GT), :]
                    own.done(dve.tensor_tensor(xs, xs, ps[:, 7, :].rearrange("p (t d) -> p t d", t=GT), ALU.add))
                    statistics(u, pre["stats"])
                    dve.wait_ge(pre["stats"], u + 1)
                    normalise(u, pre["rstd"], tokens2, pre["normed"])
                elif stage == 3:
                    dve.wait_ge(pre["logits"], u + 1)
                    lg = ps[:, 7, 0:GT * E].rearrange("p (t e) -> p t e", t=GT)

                    def over_e(a):
                        return a.unsqueeze(2).broadcast_to([P, GT, E])

                    own.done(dve.tensor_reduce(r1[:, :], lg, AX, ALU.max))
                    dve.tensor_tensor(ra[:, :, :], lg, over_e(r1[:, :]), ALU.subtract).then_inc(pre["shifted"], 1)
                    dve.wait_ge(pre["exped"], u + 1)
                    own.done(dve.tensor_reduce(r1[:, :], rb[:, :, :], AX, ALU.add))
                    own.done(dve.reciprocal(r2[:, :], r1[:, :]))
                    own.done(dve.tensor_tensor(rb[:, :, :], rb[:, :, :], over_e(r2[:, :]), ALU.mult))
                    mine = rb[:, :, :].unsqueeze(3).broadcast_to([P, GT, E, E])
                    other = rb[:, :, :].unsqueeze(2).broadcast_to([P, GT, E, E])
                    dve.tensor_tensor(cmp1[:, :, :, :], other, mine, ALU.is_gt)
                    own.done(dve.tensor_tensor(cmp2[:, :, :, :], other, mine, ALU.is_equal))
                    own.done(dve.tensor_tensor(cmp2[:, :, :, :], cmp2[:, :, :, :],
                                               lower[:, :, :].unsqueeze(1).broadcast_to([P, GT, E, E]), ALU.mult))
                    own.done(dve.tensor_tensor(cmp1[:, :, :, :], cmp1[:, :, :, :], cmp2[:, :, :, :], ALU.add))
                    own.done(dve.tensor_reduce(ra[:, :, :], cmp1[:, :, :, :], AX, ALU.add))
                    own.done(dve.scalar_tensor_tensor(rc[:, :, :], ra[:, :, :], 2.0, rb[:, :, :],
                                                      ALU.is_lt, ALU.mult))
                    own.done(dve.tensor_reduce(r1[:, :], rc[:, :, :], AX, ALU.add))
                    own.done(dve.reciprocal(r2[:, :], r1[:, :]))
                    dve.tensor_tensor(ew[:, bass.ts(u, GT), :], rc[:, :, :], over_e(r2[:, :]), ALU.mult)\
                        .then_inc(pre["weights"], 1)

            def multiply(u, e):
                for c, (f, w) in enumerate(FCH):
                    n = 3 * (E * u + e) + c
                    par = (3 * e + c) % 2
                    if c == 0 and e:
                        dve.wait_ge(moe["down"], E * u + e - 1 + AT_ONE)
                    dve.wait_ge(moe["silu"], n + 3)
                    dve.wait_ge(moe["up"], n + 1)
                    dve.tensor_tensor(acts[0:w, e % 2, c, :], ps[0:w, 2 + par, :], gated[0:w, par, :], ALU.mult)\
                        .then_inc(moe["mul"], 1)

            def accumulate(u, e):
                n = E * u + e
                dve.wait_ge(moe["down"], n + 1 + AT_ONE)
                dve.wait_ge(moe["acc"], n + 2)
                if e == 0:
                    dve.wait_ge(pre["weights"], u + 1)
                for k in range(GT):
                    xs = x[:, u * GT + k, :]
                    last = dve.scalar_tensor_tensor(xs, ps[:, 4 + e % 2, k * D:(k + 1) * D],
                                                    ew[:, u * GT + k, e:e + 1], xs, ALU.mult, ALU.add)
                last.then_inc(moe["acc"], 1)

            def experts(u, more):
                for e in range(E):
                    multiply(u, e)
                    if e:
                        accumulate(u, e - 1)
                    if more and e in (0, 3):
                        prepare(u + 1, e // 2)
                accumulate(u, E - 1)
                if more:
                    prepare(u + 1, 3)

            dve.wait_ge(x_in, 16)
            project(0)
            attention(0)
            dve.wait_ge(s[0]["attn_done"], 2 * NQ + AT_ONE)
            for stage in range(4):
                prepare(0, stage)
            chain = 2 + 11
            with dve.Fori(0, NG - 1) as u:
                own.loop(u, chain)
                experts(u, True)
            own.end_loop(NG - 1, chain)
            experts(NG - 1, False)
            dve.wait_ge(moe["acc"], E * NG + 2)
            project(1)
            attention(1)
            dve.wait_ge(s[1]["attn_done"], 2 * NQ + AT_ONE)

            with dve.Fori(0, NG) as u:
                own.loop(u, 3 + FC)
                xs = x[:, bass.ts(u, GT), :]
                dve.wait_ge(ff["a_turned"], u + AT_ONE)
                dve.tensor_copy(tokens[:, :, :], attn[:, bass.ts(u, GT), :]).then_inc(ff["attn_staged"], 1)
                dve.wait_ge(ff["wo_out"], u + 1)
                dve.wait_ge(ff["attn_staged"], u + 1)
                own.done(dve.tensor_tensor(tokens2[:, :, :], ps[:, 1, :].rearrange("p (t d) -> p t d", t=GT),
                                           tokens[:, :, :], ALU.add))
                own.done(dve.tensor_tensor(xs, xs, tokens2[:, :, :], ALU.add))
                statistics(u, ff["stats"])
                dve.wait_ge(ff["stats"], u + 1)
                normalise(u, ff["rstd"], tokens2, ff["normed"])

                def reduced(c):
                    n = FC * u + c
                    dve.wait_ge(ff["turns"], n + 1)
                    a, k = arg[:, c % 2, :], turns[:, c % 2, :]
                    own.done(dve.scalar_tensor_tensor(a, k, -C1, a, ALU.mult, ALU.add))
                    dve.scalar_tensor_tensor(a, k, -C2, a, ALU.mult, ALU.add).then_inc(ff["reduced"], 1)

                def mixed(c):
                    n = FC * u + c
                    dve.wait_ge(ff["sine"], n + 1)
                    sn = sine[:, c % 2, :]
                    dve.scalar_tensor_tensor(sn, sn, coef[:, c:c + 1], hid[:, c % 2, :], ALU.mult, ALU.add)\
                        .then_inc(ff["mixed"], 1)

                for c in range(FC):
                    reduced(c)
                    if c:
                        mixed(c - 1)
                mixed(FC - 1)
                dve.wait_ge(ff["y_out"], u + 1 + AT_ONE)
                dve.wait_ge(ff["stored"], 16 * u + AT_ONE)
                for k in range(GT):
                    last = dve.tensor_tensor(y[:, k, :], x[:, u * GT + k, :], b2r[:, :], ALU.add)
                last.then_inc(ff["added"], 1)
                dve.wait_ge(ff["added"], u + 1)
                dve.tensor_tensor(y[:, :, :], y[:, :, :], ps[:, 6, :].rearrange("p (t d) -> p t d", t=GT),
                                  ALU.add).then_inc(ff["y_ready"], 1)
            own.end_loop(NG, 3 + FC)


_INS = ["L0_attn_h", "L0_attn_Wqvk", "L0_attn_Wo", "L0_ffn_router_w", "L0_ffn_gate_proj", "L0_ffn_up_proj",
        "L0_ffn_down_proj", "L1_attn_w_q", "L1_attn_w_k", "L1_attn_w_v", "L1_attn_w_o", "L1_attn_g", "L1_ffn_W1",
        "L1_ffn_b1", "L1_ffn_quantum_phases", "L1_ffn_quantum_weights_real", "L1_ffn_quantum_weights_imag",
        "L1_ffn_W2", "L1_ffn_b2"]


def rope_table():
    i = np.arange(HD)
    theta = np.power(np.float32(10000.0), (-2.0 * (i // 2) / HD).astype(np.float32))
    angle = np.arange(S, dtype=np.float32)[:, None] * theta[None, :]
    sign = np.where(np.arange(S) % 2 == 1, -1.0, 1.0).astype(np.float32)
    factor = np.cos(angle) + sign[:, None] * np.sin(angle)
    return np.ascontiguousarray(np.tile(factor.T, (H, 1)), dtype=np.float32)


_COLUMNS = {"L1_attn_g", "L1_ffn_b1", "L1_ffn_quantum_phases", "L1_ffn_quantum_weights_real",
            "L1_ffn_quantum_weights_imag"}


def kernel(**inputs):
    import concourse.bacc as bacc
    from concourse.bass_utils import run_bass_kernel_spmd

    nc = bacc.Bacc("TRN2", target_bir_lowering=False, num_devices=1)
    arrays, args = {}, []
    for name, a in [(n, inputs[n]) for n in _INS] + [("rope", rope_table())]:
        a = np.asarray(a)
        a = np.ascontiguousarray(a.reshape(-1, P).T if name in _COLUMNS else a)
        arrays[f"in_{name}_dram"] = a
        args.append(nc.dram_tensor(f"in_{name}_dram", a.shape, mybir.dt.from_np(a.dtype), kind="ExternalInput").ap())
    out = nc.dram_tensor("out_0_dram", (B, S, D), F32, kind="ExternalOutput").ap()
    build(nc, *args, out)
    r = run_bass_kernel_spmd(nc, [arrays], core_ids=[0])
    return r.results[0]["out_0_dram"]
```

```python
from contextlib import ExitStack

import numpy as np

import concourse.bass as bass
from concourse import mybir

F32 = mybir.dt.float32
BF16 = mybir.dt.bfloat16
ALU = mybir.AluOpType
ACT = mybir.ActivationFunctionType
AX = mybir.AxisListType.X

P = 128
B, S, D = 4, 1024, 128
H, HD, KV = 16, 8, 4
T = B * S // P
GT = 4
NG = T // GT
GW = GT * P
E, F0 = 8, 352
FCH = [(0, 128), (128, 128), (256, 96)]
F1 = 512
FC = F1 // P
LN_EPS = 1e-5
RMS_EPS = float(np.finfo(np.float32).eps)
SCALE = 1.0 / float(np.sqrt(D))
MASKED = -1e30

NQ = B * 4
SPL = 3
CROSS = SPL * SPL * HD
KROWS = CROSS + SPL
SLOTS = 4
PR = 8
HALF = 512

TWO_PI = 2.0 * np.pi
C1 = 6.28125
C2 = float(TWO_PI - C1)
ROUND = 12582912.0
PI_IN = 3.1415925


AT_ONE = 1


class Chain:

    def __init__(self, eng, sem, own_wait=False):
        self.eng, self.sem, self.start, self.n, self.own_wait = eng, sem, 0, 0, own_wait

    def done(self, ins):
        self.n += 1
        ins.then_inc(self.sem, 1)
        self.eng.wait_ge(self.sem, self.start + self.n)
        if self.own_wait:
            self.eng.nop(nofuse=True)

    def loop(self, turn, each):
        self.first = self.start + self.n
        self.start, self.n = self.first + turn * each, 0

    def end_loop(self, turns, each):
        assert self.n == each, (self.n, each)
        self.start, self.n = self.first + turns * each, 0


class Heads:

    def __init__(self, causal, letters):
        self.causal = causal
        self.groups = [(h, t) for h in range(2) for t in range(8) if not causal or t // 4 <= h]
        self.G = len(self.groups)
        self.last_of_half = [max(m for m, (h, _) in enumerate(self.groups) if h == half) for half in range(2)]
        self.events = self.order(letters)

    def cols(self, m):
        h, t = self.groups[m]
        return max(0, P * t - HALF * h) if self.causal else 0

    def diagonal(self, m):
        h, t = self.groups[m]
        return self.causal and t // 4 == h

    def keys(self, i):
        return P * (i + 1) if self.causal else S

    def order(self, letters):
        out, count = [], dict.fromkeys("abpmsctn", 0)
        for letter in letters:
            n = count[letter]
            count[letter] += 1
            if letter == "b":
                out.append(("B", n // 4, n % 4))
            elif letter == "a":
                out.append(("A", n))
            elif letter == "p":
                out.append(("PV", n))
            elif letter == "m":
                out.append(("MT", count["n"]))
            elif letter == "s":
                out.append(("MC",))
            elif letter == "t":
                out.append(("OT", n, count["s"]))
            else:
                out.append(({"c": "OC", "n": "ON"}[letter], n))
        assert list(count.values()) == [32, 4 * self.G, self.G, 1, 1, 2, 2, 2]
        return out


ORDERS = [
    "bbabbabababpbbaabbpbbaabbpbbbapbacabbatbababpbbnaabbpbabpababababababpbababpbabpbabmsababbabbppaactn",
    "bbbbabbpbbaabbpbbaabbpbbaabbpbbaabbpbbaabbpbbaabbpbbaabbpcbabtbabanbpbbpbbaabbpbbaabbpbababbpbbaabbpbbabmasbbapbbapcaatn",
]
LAYERS = [Heads(True, ORDERS[0]), Heads(False, ORDERS[1])]
QUAD_LOADS = 2 * SPL * SPL + 1


def build(nc, h_in, Wqvk, Wo0, router_w, gate_proj, up_proj, down_proj, w_q, w_k, w_v, w_o, g_rms,
          W1, b1, phases, w_real, w_imag, W2, b2, rope, out):
    q_parts = [nc.dram_tensor(f"q_parts{l}", (SPL, P, B * S), BF16, kind="Internal").ap() for l in range(2)]
    k_parts = [nc.dram_tensor(f"k_parts{l}", (SPL, r, B * S), BF16, kind="Internal").ap()
               for l, r in enumerate((P, KV * HD))]
    x_dram = h_in.rearrange("b (t p) d -> p (b t) d", p=P)
    out_dram = out.rearrange("b (t p) d -> p (b t) d", p=P)

    with ExitStack() as ctx:
        def sb(name, shape, dt=F32):
            return ctx.enter_context(nc.sbuf_tensor(name, shape, dt))

        def sem(name):
            return ctx.enter_context(nc.semaphore(name))

        x = sb("x", [P, T, D])
        attn = sb("attn", [P, T, D])
        v1 = sb("v1", [P, T, H * (HD + 1)])
        Q = sb("Q", [P, SLOTS, 4, S], BF16)
        K = sb("K", [P, SLOTS, 4, S], BF16)
        V = sb("V", [P, SLOTS, 8, 4 * (HD + 1)])
        probs = sb("probs", [P, PR, HALF])
        oT = sb("oT", [P, HALF])
        rowmax = sb("rowmax", [P, 2, 32])
        negmax = sb("negmax", [P, SPL, 32], BF16)
        negrest = sb("negrest", [P, 32])
        negmaxT = sb("negmaxT", [SPL * 32, P], BF16)
        rden = sb("rden", [P, 4, 4])
        spare = Q[:, :, :, :].rearrange("p s j n -> p (s j n)").bitcast(F32)
        hT_all = spare[:, 0:B * S]
        acts = spare[:, B * S:B * S + 6 * GW].rearrange("p (a c n) -> p a c n", a=2, c=len(FCH))
        gated = spare[:, B * S + 6 * GW:B * S + 8 * GW].rearrange("p (a n) -> p a n", a=2)
        act1 = spare[:, B * S:B * S + FC * GW].rearrange("p (c n) -> p c n", c=FC)
        spare_k = K[:, :, :, :].rearrange("p s j n -> p (s j n)").bitcast(F32)
        hid, arg, turns = (spare_k[:, n * FC * GW:(n + 1) * FC * GW].rearrange("p (c n) -> p c n", c=FC)
                           for n in range(3))
        ident = sb("ident", [P, P])
        identb = sb("identb", [P, P], BF16)
        causal = sb("causal", [P, P], BF16)
        wqvk = sb("wqvk", [P, 3 * D])
        wo0 = sb("wo0", [P, D])
        wr = sb("wr", [P, E])
        wg = sb("wg", [P, E, F0])
        wu = sb("wu", [P, E, F0])
        wd = sb("wd", [P, len(FCH), E, D])
        wq1 = sb("wq1", [P, D])
        wk1 = sb("wk1", [P, KV * HD])
        wv1 = sb("wv1", [P, KV * HD])
        wo1 = sb("wo1", [P, D])
        gcol = sb("gcol", [P, 1])
        w1 = sb("w1", [P, F1])
        w2 = sb("w2", [P, FC, D])
        b1c = sb("b1c", [P, FC])
        th = sb("th", [P, FC])
        wrl = sb("wrl", [P, FC])
        wim = sb("wim", [P, FC])
        b2r = sb("b2r", [P, D])
        ropeT = sb("ropeT", [P, S])
        stats = sb("stats", [P, GT, 6])
        mv = sb("mv", [P, GT, 2])
        rstd = sb("rstd", [P, GT])
        rtmp = sb("rtmp", [P, GT])
        rms = sb("rms", [P, GT])
        power = sb("power", [P, GT])
        tokens = sb("tokens", [P, GT, D])
        tokens2 = sb("tokens2", [P, GT, D])
        hT = sb("hT", [P, GW])
        aT = sb("aT", [P, GW])
        qk32 = probs[:, 0:2, :]
        rest = probs[:, 2:4, :]
        parts = probs[:, 4:7, :].rearrange("p a n -> p (a n)").bitcast(BF16)\
            .rearrange("p (a c n) -> p a c n", a=2, c=SPL)
        ew = sb("ew", [P, T, E])
        lower = sb("lower", [P, E, E])
        ra = sb("ra", [P, GT, E])
        rb = sb("rb", [P, GT, E])
        rc = sb("rc", [P, GT, E])
        r1 = sb("r1", [P, GT])
        r2 = sb("r2", [P, GT])
        cmp1 = sb("cmp1", [P, GT, E, E])
        cmp2 = sb("cmp2", [P, GT, E, E])
        tc1 = sb("tc1", [P, FC])
        tc2 = sb("tc2", [P, FC])
        thr = sb("thr", [P, FC])
        thc = sb("thc", [P, FC])
        sin_th = sb("sin_th", [P, FC])
        cos_th = sb("cos_th", [P, FC])
        coef = sb("coef", [P, FC])
        argb = sb("argb", [P, FC])
        y = sb("y", [P, GT, D])

        ps = ctx.enter_context(nc.psum_tensor("ps", [P, 8, 512], F32))
        def score_a(n):
            return ps[:, 2 * n:2 * n + 2, :].rearrange("p b n -> p (b n)")

        PV_BANK, MISC = 6, 7

        x_in, w_in = sem("x_in"), sem("w_in")
        consts = sem("consts")
        vec, pool_own = sem("vector_own"), sem("gpsimd_own")
        names = ("normed", "turned", "h_ready", "stats_ready", "rstd_ready", "q_out", "k_out", "v_out", "qk_sb",
                 "v_taken", "split_done", "parts_written", "scores", "max_done", "negmax_ready", "negmaxT_psum",
                 "negmaxT_ready", "negmax_rows", "scoresT", "exp_done", "pv_done", "o_copied", "o_turned",
                 "attn_done")
        from_one = ("h_ready", "v_out", "qk_sb", "v_taken", "split_done", "parts_written", "o_copied", "o_turned",
                    "attn_done")
        s = [{n: sem(f"{n}{l}") for n in names} for l in range(2)]
        loaded = [[sem(f"loaded{l}_{k}") for k in range(SLOTS)] for l in range(2)]
        pre = {n: sem("pre_" + n) for n in
               ("attn_staged", "a_turned", "a_ready", "wo_out", "stats", "rstd", "normed", "turned", "h_ready",
                "logits", "shifted", "exped", "weights")}
        moe = {n: sem("moe_" + n) for n in ("gate", "up", "silu", "mul", "down", "acc")}
        ff = {n: sem("ff_" + n) for n in
              ("attn_staged", "a_turned", "a_ready", "wo_out", "added", "stats", "rstd", "normed", "turned", "h_ready",
               "hidden", "arg", "hid", "turns", "reduced", "sine", "mixed", "relu", "y_out", "y_ready", "stored")}
        theta = {n: sem("theta_" + n) for n in ("reduced", "sines", "coef")}

        weights = [
            (wqvk[:, :], Wqvk), (wo0[:, :], Wo0), (wr[:, :], router_w),
            (wg[:, :, :], gate_proj.rearrange("e d f -> d e f")), (wu[:, :, :], up_proj.rearrange("e d f -> d e f")),
            *[(wd[0:w, c, :, :], down_proj[:, f:f + w, :].rearrange("e f d -> f e d")) for c, (f, w) in enumerate(FCH)],
            (wq1[:, :], w_q), (wk1[:, :], w_k), (wv1[:, :], w_v), (wo1[:, :], w_o), (gcol[:, :], g_rms),
            (w1[:, :], W1), (w2[:, :, :], W2.rearrange("(c p) d -> p c d", p=P)), (b1c[:, :], b1),
            (th[:, :], phases), (wrl[:, :], w_real), (wim[:, :], w_imag),
            (b2r[:, :], b2.rearrange("(a d) -> a d", a=1).broadcast_to([P, D])), (ropeT[:, :], rope),
        ]

        starting = [s[l][n] for l in range(2) for n in from_one] + [moe["down"]] + \
            [ff[n] for n in ("arg", "y_ready", "a_turned", "stored")]

        block = ctx.enter_context(nc.Block())

        def apart(eng):
            eng.nop(nofuse=True)

        @block.sync
        def _(sp):
            sp.dma_start(x[:, :, :], x_dram).then_inc(x_in, 16)
            for semaphore in starting:
                sp.sem_inc(semaphore, 1)
            sp.sem_inc(ff["y_out"], FC)
            for l in range(2):
                sl = s[l]
                rows_k = P if l == 0 else KV * HD

                with sp.Fori(0, NG) as u:
                    sp.wait_ge(sl["split_done"], 2 * u + 2 + AT_ONE)
                    sp.dma_start(q_parts[l][:, :, bass.ts(u, GW)].rearrange("c p n -> p c n"),
                                 parts[:, 0, :, :]).then_inc(sl["parts_written"], 16)
                    sp.dma_start(k_parts[l][:, :, bass.ts(u, GW)].rearrange("c p n -> p c n"),
                                 parts[0:rows_k, 1, :, :]).then_inc(sl["parts_written"], 16)
                sp.wait_ge(sl["parts_written"], 32 * NG + AT_ONE)

                def load(b, q):
                    for a in range(SPL):
                        heads = q_parts[l][a, :, bass.ts(b, S)].rearrange("(h i) n -> i h n", i=HD)
                        heads = heads[:, 4 * q:4 * q + 4, :] if l == 0 else heads[:, q:H:KV, :]
                        for r in range(SPL):
                            row = (a * SPL + r) * HD
                            sp.dma_start(Q[row:row + HD, q, :, :], heads).then_inc(loaded[l][q], 16)
                            keys = k_parts[l][r, :, bass.ts(b, S)].rearrange("(h i) n -> i h n", i=HD)
                            keys = keys[:, 4 * q:4 * q + 4, :] if l == 0 else keys[:, q:q + 1, :]
                            sp.dma_start(K[row:row + HD, q, 0:keys.shape[1], :], keys).then_inc(loaded[l][q], 16)
                    w = (HD + 1) * (4 if l == 0 else 1)
                    sp.dma_start(V[:, q, :, 0:w], v1[:, bass.ts(b, 8), w * q:w * q + w]).then_inc(loaded[l][q], 16)

                def negmax_rows(q, g):
                    sp.wait_ge(sl["negmaxT_ready"], g + 1)
                    for c in range(SPL):
                        sp.dma_start(Q[CROSS + c:CROSS + c + 1, q, :, :].rearrange("c j (i n) -> c (j i) n", n=P),
                                     negmaxT[32 * c:32 * c + 32, :]).then_inc(sl["negmax_rows"], 16)

                sp.wait_ge(consts, 6)
                sp.wait_ge(sl["v_taken"], NG + AT_ONE)
                for q in range(3):
                    load(0, q)
                negmax_rows(0, 0)

                def batch(b, final):
                    for q in range(4):
                        g = 4 * b + q
                        if q == 0 or not final:
                            sp.wait_ge(sl["o_turned"], 2 * g + AT_ONE)
                            load(b if q == 0 else b + 1, (q + 3) % 4)
                        if q < 3 or not final:
                            negmax_rows((q + 1) % 4, g + 1)

                with sp.Fori(0, B - 1) as b:
                    batch(b, False)
                batch(B - 1, True)

            with sp.Fori(0, NG) as u:
                sp.wait_ge(ff["y_ready"], u + 1 + AT_ONE)
                sp.dma_start(out_dram[:, bass.ts(u, GT), :], y[:, :, :]).then_inc(ff["stored"], 16)
            sp.wait_ge(ff["stored"], 16 * NG + AT_ONE)

        @block.gpsimd
        def _(pool):
            own = Chain(pool, pool_own, own_wait=True)
            own.done(pool.memset(ident[:, :], 0.0))
            own.done(pool.memset(identb[:, :], 0.0))
            own.done(pool.memset(causal[:, :], 0.0))
            own.done(pool.memset(lower[:, :, :], 0.0))
            own.done(pool.memset(power[:, :], -0.5))
            for m in (ident, identb):
                pool.affine_select(out=m[:, :], in_=m[:, :], compare_op=ALU.not_equal, fill=1.0, base=0,
                                   pattern=[[-1, P]], channel_multiplier=1).then_inc(consts, 1)
            pool.affine_select(out=causal[:, :], in_=causal[:, :], compare_op=ALU.is_ge, fill=MASKED, base=0,
                               pattern=[[-1, P]], channel_multiplier=1).then_inc(consts, 1)
            pool.affine_select(out=lower[:, :, :], in_=lower[:, :, :], compare_op=ALU.is_ge, fill=1.0, base=0,
                               pattern=[[-1, E], [1, E]], channel_multiplier=0).then_inc(consts, 1)
            own.done(pool.memset(v1[:, :, :], 1.0))
            pool.memset(K[64:96, :, :, :], 1.0).then_inc(consts, 1)

            def inverse(ready, done, u, with_rms=False):
                pool.wait_ge(ready, u + 1)
                apart(pool)
                if not with_rms:
                    own.done(pool.tensor_scalar(rtmp[:, :], mv[:, :, 1], LN_EPS, 1.0, ALU.add, ALU.mult))
                    pool.tensor_tensor(rstd[:, :], rtmp[:, :], power[:, :], ALU.pow).then_inc(done, 1)
                    return
                own.done(pool.tensor_scalar(rtmp[:, :], mv[:, :, 1], LN_EPS, 1.0, ALU.add, ALU.mult))
                own.done(pool.tensor_tensor(rms[:, :], rtmp[:, :], power[:, :], ALU.pow))
                own.done(pool.tensor_tensor(rtmp[:, :], mv[:, :, 1], rms[:, :], ALU.mult))
                own.done(pool.tensor_tensor(rtmp[:, :], rtmp[:, :], rms[:, :], ALU.mult))
                own.done(pool.tensor_scalar(rtmp[:, :], rtmp[:, :], RMS_EPS, 1.0, ALU.add, ALU.mult))
                own.done(pool.tensor_tensor(rtmp[:, :], rtmp[:, :], power[:, :], ALU.pow))
                pool.tensor_tensor(rstd[:, :], rms[:, :], rtmp[:, :], ALU.mult).then_inc(done, 1)

            with pool.Fori(0, NG) as u:
                own.loop(u, 1)
                inverse(s[0]["stats_ready"], s[0]["rstd_ready"], u)
            own.end_loop(NG, 1)
            with pool.Fori(0, NG) as u:
                own.loop(u, 1)
                inverse(pre["stats"], pre["rstd"], u)
            own.end_loop(NG, 1)
            with pool.Fori(0, NG) as u:
                own.loop(u, 6)
                inverse(s[1]["stats_ready"], s[1]["rstd_ready"], u, True)
            own.end_loop(NG, 6)

            def turn_counts(u, c):
                pool.wait_ge(ff["arg"], FC * u + c + 1 + AT_ONE)
                apart(pool)
                own.done(pool.tensor_scalar(turns[:, c, :], arg[:, c, :], 1.0, ROUND, ALU.mult, ALU.add))
                pool.tensor_scalar(turns[:, c, :], turns[:, c, :], -ROUND, 1.0,
                                   ALU.add, ALU.mult).then_inc(ff["turns"], 1)

            def add_b2(u):
                pool.wait_ge(ff["stored"], 16 * u + AT_ONE)
                pool.tensor_tensor(y[:, :, :], x[:, bass.ts(u, GT), :],
                                   b2r[:, :].unsqueeze(1).broadcast_to([P, GT, D]), ALU.add)\
                    .then_inc(ff["added"], 1)

            def feed_forward(u, before=True, now=True, following=True, more=True):
                for c in range(FC):
                    if now:
                        turn_counts(u, c)
                    if c == 2 and more:
                        inverse(ff["stats"], ff["rstd"], u + 2)
                    if c == 1 and before:
                        add_b2(u - 1)

            inverse(ff["stats"], ff["rstd"], 0)
            inverse(ff["stats"], ff["rstd"], 1)
            feed_forward(0, before=False)
            with pool.Fori(0, NG - 3) as v:
                own.loop(v, 1 + FC)
                feed_forward(v + 1)
            own.end_loop(NG - 3, 1 + FC)
            feed_forward(NG - 2, more=False)
            feed_forward(NG - 1, following=False, more=False)
            feed_forward(NG, now=False, following=False, more=False)

        @block.tensor
        def _(pe):
            def turn(src, bank, done):
                for k in range(GT):
                    last = pe.transpose(ps[:, bank, k * P:(k + 1) * P], src[:, k, :], ident[:, :])
                last.then_inc(done, 1)

            def project(l):
                sl = s[l]
                with pe.Fori(0, NG) as u:
                    pe.wait_ge(sl["normed"], u + 1)
                    pe.wait_ge(sl["h_ready"], u + AT_ONE)
                    turn(tokens, 0, sl["turned"])
                    pe.wait_ge(sl["h_ready"], u + 1 + AT_ONE)
                    pe.wait_ge(sl["qk_sb"], 2 * u + AT_ONE)
                    pe.wait_ge(sl["v_taken"], u + AT_ONE)
                    if l == 0:
                        wq, wv, wk = (wqvk[:, n * D:(n + 1) * D] for n in range(3))
                        rk, wd_v = P, D
                    else:
                        wq, wk, wv, rk, wd_v = wq1[:, :], wk1[:, :], wv1[:, :], KV * HD, KV * HD
                    pe.matmul(ps[:, 1, :], wq, hT[:, :], start=True, stop=True).then_inc(sl["q_out"], 1)
                    pe.matmul(ps[0:rk, 2, :], wk, hT[:, :], start=True, stop=True).then_inc(sl["k_out"], 1)
                    for k in range(GT):
                        last = pe.matmul(ps[:, 3, k * wd_v:(k + 1) * wd_v], hT[:, k * P:(k + 1) * P], wv,
                                         start=True, stop=True)
                    last.then_inc(sl["v_out"], 1)

            def attention(l):
                sl, hd = s[l], LAYERS[l]
                G, nB = hd.G, 4 * hd.G
                rows = HD + 1

                def pass_a(quad, slot, j, i):
                    n = 32 * quad + 8 * j + i
                    buf = score_a(i % 2)
                    kj = j if l == 0 else 0
                    if not isinstance(n, int) or n >= 2:
                        pe.wait_ge(sl["max_done"], n - 1)
                    w = hd.keys(i)
                    for c in range(0, w, 512):
                        e = min(c + 512, w)
                        diag = hd.causal and e == w
                        last = pe.matmul(buf[:, c:e], Q[0:CROSS, slot, j, i * P:(i + 1) * P],
                                         K[0:CROSS, slot, kj, c:e], start=True, stop=not diag)
                        if diag:
                            last = pe.matmul(buf[:, w - P:w], identb[:, :], causal[:, :],
                                             start=False, stop=True)
                    last.then_inc(sl["scores"], 1)

                def pass_b(g, q, m, j):
                    n = nB * g + 4 * m + j
                    h, t = hd.groups[m]
                    c = hd.cols(m)
                    pe.wait_ge(sl["exp_done"], n + 1)
                    kj = j if l == 0 else 0
                    diag = hd.diagonal(m)
                    last = pe.matmul(ps[:, 4 + j % 2, c:HALF], K[0:KROWS, q, kj, t * P:(t + 1) * P],
                                     Q[0:KROWS, q, j, h * HALF + c:(h + 1) * HALF], start=True, stop=not diag)
                    if diag:
                        last = pe.matmul(ps[:, 4 + j % 2, c:c + P], causal[:, :], identb[:, :],
                                         start=False, stop=True)
                    last.then_inc(sl["scoresT"], 1)

                def pv(g, q, m):
                    h, t = hd.groups[m]
                    c = hd.cols(m)
                    if t == 0:
                        pe.wait_ge(sl["o_copied"], 2 * g + h + AT_ONE)
                    for j in range(4):
                        n = nB * g + 4 * m + j
                        pe.wait_ge(sl["exp_done"], n + 3)
                        kj = j if l == 0 else 0
                        last = pe.matmul(ps[32 * j:32 * j + rows, PV_BANK, c:HALF],
                                         V[:, q, t, kj * rows:(kj + 1) * rows],
                                         probs[:, (4 * m + j) % PR, c:HALF],
                                         start=(t == 0), stop=(m == hd.last_of_half[h]), skip_group_check=True)
                    last.then_inc(sl["pv_done"], 1)

                def negmax_turn(g, g_prev_norms):
                    pe.wait_ge(sl["negmax_ready"], g + 1)
                    pe.wait_ge(sl["attn_done"], g_prev_norms + AT_ONE)
                    pe.transpose(ps[0:SPL * 32, MISC, 0:P // 2].bitcast(BF16),
                                 negmax[:, :, :].rearrange("p c n -> p (c n)"), identb[:, :])\
                        .then_inc(sl["negmaxT_psum"], 1)

                def out_turn(g, h, turned_max):
                    pe.wait_ge(sl["o_copied"], 2 * g + h + 1 + AT_ONE)
                    pe.wait_ge(sl["attn_done"], 2 * g + h + AT_ONE)
                    pe.wait_ge(sl["negmaxT_ready"], turned_max)
                    for k in range(4):
                        last = pe.transpose(ps[:, MISC, k * P:(k + 1) * P], oT[:, k * P:(k + 1) * P], ident[:, :])
                    last.then_inc(sl["o_turned"], 1)

                def quad_loaded(b, q):
                    pe.wait_ge(loaded[l][q], 16 * QUAD_LOADS * (b + 1))

                quad_loaded(0, 0)
                for n in range(32):
                    pass_a(0, 0, n // 8, n % 8)
                quad_loaded(0, 1)
                for n in range(8):
                    pass_a(1, 1, 0, n)
                negmax_turn(0, 0)

                def batch(b, final):
                    for q in range(4):
                        g = 4 * b + q
                        more_1, more_2 = not (final and q == 3), not (final and q >= 2)
                        pe.wait_ge(sl["negmax_rows"], 16 * SPL * (g + 1))
                        for ev in hd.events:
                            if ev[0] == "B":
                                pass_b(g, q, ev[1], ev[2])
                            elif ev[0] == "A":
                                k = ev[1]
                                if k < 24 and more_1:
                                    pass_a(g + 1, (q + 1) % 4, 1 + k // 8, k % 8)
                                if k >= 24 and more_2:
                                    if k == 24:
                                        quad_loaded(b + (q >= 2), (q + 2) % 4)
                                    pass_a(g + 2, (q + 2) % 4, 0, k % 8)
                            elif ev[0] == "PV":
                                pv(g, q, ev[1])
                            elif ev[0] == "MT" and more_1:
                                negmax_turn(g + 1, 2 * g + ev[1])
                            elif ev[0] == "OT":
                                out_turn(g, ev[1], g + 1 + (ev[2] if more_1 else 0))

                with pe.Fori(0, B - 1) as b:
                    batch(b, False)
                batch(B - 1, True)

            def prepare(u, stage):
                if stage == 0:
                    pe.wait_ge(pre["attn_staged"], u + 1)
                    pe.wait_ge(pre["h_ready"], u)
                    turn(tokens, 6, pre["a_turned"])
                elif stage == 1:
                    pe.wait_ge(pre["a_ready"], u + 1)
                    pe.wait_ge(pre["weights"], u)
                    for k in range(GT):
                        last = pe.matmul(ps[:, 7, k * D:(k + 1) * D], aT[:, k * P:(k + 1) * P], wo0[:, :],
                                         start=True, stop=True)
                    last.then_inc(pre["wo_out"], 1)
                elif stage == 2:
                    pe.wait_ge(pre["normed"], u + 1)
                    turn(tokens2, 6, pre["turned"])
                else:
                    pe.wait_ge(pre["h_ready"], u + 1)
                    for k in range(GT):
                        last = pe.matmul(ps[:, 7, k * E:(k + 1) * E], hT[:, k * P:(k + 1) * P], wr[:, :],
                                         start=True, stop=True)
                    last.then_inc(pre["logits"], 1)

            def gate_up(u, e):
                for c, (f, w) in enumerate(FCH):
                    n = 3 * (E * u + e) + c
                    par = (3 * e + c) % 2
                    moving = hT_all[:, bass.ts(u, GW)]
                    pe.wait_ge(moe["silu"], n + 1)
                    pe.matmul(ps[0:w, par, :], wg[:, e, f:f + w], moving,
                              start=True, stop=True).then_inc(moe["gate"], 1)
                    pe.wait_ge(moe["mul"], n + 1)
                    pe.matmul(ps[0:w, 2 + par, :], wu[:, e, f:f + w], moving,
                              start=True, stop=True).then_inc(moe["up"], 1)

            def down(u, e):
                n = E * u + e
                pe.wait_ge(moe["mul"], 3 * n + 5)
                pe.wait_ge(moe["acc"], n + 1)
                for k in range(GT):
                    for c, (f, w) in enumerate(FCH):
                        last = pe.matmul(ps[:, 4 + e % 2, k * D:(k + 1) * D],
                                         acts[0:w, e % 2, c, k * P:(k + 1) * P], wd[0:w, c, e, :],
                                         start=(c == 0), stop=(c == len(FCH) - 1))
                last.then_inc(moe["down"], 1)

            def experts(u, more):
                for e in range(E):
                    gate_up(u, e)
                    if e:
                        down(u, e - 1)
                    if more and e % 2:
                        prepare(u + 1, e // 2)
                down(u, E - 1)

            def ff_prepare(u, stage):
                if stage == 0:
                    pe.wait_ge(ff["attn_staged"], u + 1)
                    turn(tokens, 0, ff["a_turned"])
                elif stage == 1:
                    pe.wait_ge(ff["a_ready"], u + 1)
                    for k in range(GT):
                        pe.matmul(ps[:, 1, k * D:(k + 1) * D], aT[:, k * P:(k + 1) * P], wo1[:, :],
                                  start=True, stop=False)
                        last = pe.matmul(ps[:, 1, k * D:(k + 1) * D], aT[:, k * P:(k + 1) * P], ident[:, :],
                                         start=False, stop=True)
                    last.then_inc(ff["wo_out"], 1)
                else:
                    pe.wait_ge(ff["normed"], u + 1)
                    turn(tokens2, 7, ff["turned"])

            def ff_hidden(u, c):
                if c == 0:
                    pe.wait_ge(ff["h_ready"], u + 1)
                if not isinstance(u, int) or u > 0:
                    pe.wait_ge(ff["hid"], FC * u + c + 1 - FC)
                pe.matmul(ps[:, 2 + c, :], w1[:, c * P:(c + 1) * P], hT_all[:, bass.ts(u, GW)],
                          start=True, stop=True).then_inc(ff["hidden"], 1)

            def ff_out(u, c):
                pe.wait_ge(ff["relu"], FC * u + c + 1)
                if c == 0:
                    pe.wait_ge(ff["y_ready"], u + AT_ONE)
                for k in range(GT):
                    last = pe.matmul(ps[:, 6, k * D:(k + 1) * D], act1[:, c, k * P:(k + 1) * P], w2[:, c, :],
                                     start=(c == 0 and k == 0), stop=(c == FC - 1), skip_group_check=True)
                last.then_inc(ff["y_out"], 1)

            def feed_forward(u, before=True, now=True, following=True, more=True):
                if now:
                    ff_hidden(u, 0)
                    ff_hidden(u, 1)
                if following:
                    ff_prepare(u + 1, 2)
                if more:
                    ff_prepare(u + 2, 0)
                if before:
                    ff_out(u - 1, 1)
                if now:
                    ff_hidden(u, 2)
                if more:
                    ff_prepare(u + 2, 1)
                if now:
                    ff_hidden(u, 3)
                if before:
                    ff_out(u - 1, 2)
                    ff_out(u - 1, 3)
                if now:
                    ff_out(u, 0)

            pe.wait_ge(consts, 6)
            pe.wait_ge(w_in, 16 * len(weights))
            project(0)
            attention(0)
            for stage in range(4):
                prepare(0, stage)
            with pe.Fori(0, NG - 1) as u:
                experts(u, True)
            experts(NG - 1, False)
            project(1)
            attention(1)
            for stage in range(3):
                ff_prepare(0, stage)
            for stage in range(2):
                ff_prepare(1, stage)
            feed_forward(0, before=False)
            with pe.Fori(0, NG - 3) as v:
                feed_forward(v + 1)
            feed_forward(NG - 2, more=False)
            feed_forward(NG - 1, following=False, more=False)
            feed_forward(NG, now=False, following=False, more=False)

        @block.scalar
        def _(act):
            for dst, src in weights:
                act.dma_start(dst, src).then_inc(w_in, 16)
            act.sem_inc(moe["silu"], 2)
            for l in range(2):
                act.sem_inc(s[l]["exp_done"], 2)
            act.wait_ge(consts, 6)
            act.wait_ge(w_in, 16 * len(weights))

            act.wait_ge(theta["reduced"], 1)
            act.activation(sin_th[:, :], thr[:, :], ACT.Sin).then_inc(theta["sines"], 1)
            act.activation(cos_th[:, :], thc[:, :], ACT.Sin).then_inc(theta["sines"], 1)

            def project(l):
                sl = s[l]
                with act.Fori(0, NG) as u:
                    act.wait_ge(sl["turned"], u + 1)
                    act.wait_ge(sl["v_out"], u + AT_ONE)
                    if l == 0:
                        act.activation(hT[:, :], ps[:, 0, :], ACT.Copy).then_inc(sl["h_ready"], 1)
                    else:
                        act.activation(hT[:, :], ps[:, 0, :], ACT.Copy, scale=gcol[:, 0:1])\
                            .then_inc(sl["h_ready"], 1)
                    if l == 0:
                        act.wait_ge(sl["split_done"], 2 * u + AT_ONE)
                        act.wait_ge(sl["q_out"], u + 1)
                        act.activation(qk32[:, 0, :], ps[:, 1, :], ACT.Copy).then_inc(sl["qk_sb"], 1)
                        act.wait_ge(sl["k_out"], u + 1)
                        act.activation(qk32[:, 1, :], ps[:, 2, :], ACT.Copy).then_inc(sl["qk_sb"], 1)
                    nh = H if l == 0 else KV
                    act.wait_ge(sl["v_out"], u + 1 + AT_ONE)
                    act.activation(v1[:, bass.ts(u, GT), 0:nh * (HD + 1)]
                                   .rearrange("p t (h i) -> p t h i", i=HD + 1)[:, :, :, 0:HD],
                                   ps[:, 3, 0:GT * nh * HD].rearrange("p (t h i) -> p t h i", t=GT, i=HD),
                                   ACT.Copy).then_inc(sl["v_taken"], 1)

            def attention(l):
                sl, hd = s[l], LAYERS[l]
                G, nB = hd.G, 4 * hd.G

                def negmax_copy(g):
                    act.wait_ge(sl["negmaxT_psum"], g + 1)
                    if not isinstance(g, int) or g > 0:
                        act.wait_ge(sl["negmax_rows"], 16 * SPL * g)
                    act.activation(negmaxT[:, :], ps[0:SPL * 32, MISC, 0:P // 2].bitcast(BF16),
                                   ACT.Copy).then_inc(sl["negmaxT_ready"], 1)

                negmax_copy(0)

                def batch(b, final):
                    for q in range(4):
                        g = 4 * b + q
                        for ev in hd.events:
                            if ev[0] == "B":
                                m, j = ev[1], ev[2]
                                n = nB * g + 4 * m + j
                                c = hd.cols(m)
                                act.wait_ge(sl["scoresT"], n + 1)
                                if j == 0:
                                    act.wait_ge(sl["pv_done"], G * g + m + 1)
                                act.activation(probs[:, (4 * m + j) % PR, c:HALF], ps[:, 4 + j % 2, c:HALF],
                                               ACT.Exp, scale=SCALE).then_inc(sl["exp_done"], 1)
                            elif ev[0] == "OC":
                                act.wait_ge(sl["pv_done"], G * g + hd.last_of_half[ev[1]] + 3)
                                act.activation(oT[:, :], ps[:, PV_BANK, :], ACT.Copy)\
                                    .then_inc(sl["o_copied"], 1)
                            elif ev[0] == "MC" and not (final and q == 3):
                                negmax_copy(g + 1)

                with act.Fori(0, B - 1) as b:
                    batch(b, False)
                batch(B - 1, True)

            def prepare(u, stage):
                if stage == 0:
                    act.wait_ge(pre["a_turned"], u + 1)
                    act.activation(aT[:, :], ps[:, 6, :], ACT.Copy).then_inc(pre["a_ready"], 1)
                elif stage == 2:
                    act.wait_ge(pre["turned"], u + 1)
                    act.wait_ge(pre["logits"], u)
                    act.activation(hT[:, :], ps[:, 6, :], ACT.Copy)
                    act.activation(hT_all[:, bass.ts(u, GW)], ps[:, 6, :], ACT.Copy).then_inc(pre["h_ready"], 1)
                elif stage == 3:
                    act.wait_ge(pre["shifted"], u + 1)
                    act.activation(rb[:, :, :], ra[:, :, :], ACT.Exp).then_inc(pre["exped"], 1)

            def experts(u, more):
                for e in range(E):
                    for c, (f, w) in enumerate(FCH):
                        n = 3 * (E * u + e) + c
                        par = (3 * e + c) % 2
                        act.wait_ge(moe["gate"], n + 1)
                        act.wait_ge(moe["mul"], n + 1)
                        act.activation(gated[0:w, par, :], ps[0:w, par, :], ACT.Silu).then_inc(moe["silu"], 1)
                    if more and e in (1, 5, 7):
                        prepare(u + 1, e // 2)

            project(0)
            attention(0)
            for stage in range(4):
                prepare(0, stage)
            with act.Fori(0, NG - 1) as u:
                experts(u, True)
            experts(NG - 1, False)
            project(1)
            attention(1)

            def ff_prepare(u, stage):
                if stage == 0:
                    act.wait_ge(ff["a_turned"], u + 1 + AT_ONE)
                    act.activation(aT[:, :], ps[:, 0, :], ACT.Copy).then_inc(ff["a_ready"], 1)
                else:
                    act.wait_ge(ff["turned"], u + 1)
                    act.activation(hT_all[:, bass.ts(u, GW)], ps[:, 7, :], ACT.Copy).then_inc(ff["h_ready"], 1)

            def hidden(u, c):
                act.wait_ge(ff["hidden"], FC * u + c + 1)
                if not isinstance(u, int) or u > 0:
                    act.wait_ge(ff["relu"], FC * u + c + 1 - FC)
                act.activation(arg[:, c, :], ps[:, 2 + c, :], ACT.Identity, bias=argb[:, c:c + 1],
                               scale=0.1 / TWO_PI).then_inc(ff["arg"], 1)
                act.activation(hid[:, c, :], ps[:, 2 + c, :], ACT.Identity, bias=b1c[:, c:c + 1])\
                    .then_inc(ff["hid"], 1)

            def sines(u, c):
                act.wait_ge(ff["reduced"], FC * u + c + 1)
                act.activation(arg[:, c, :], arg[:, c, :], ACT.Sin, scale=2.0 * PI_IN).then_inc(ff["sine"], 1)

            def relu(u, c):
                act.wait_ge(ff["mixed"], FC * u + c + 1)
                act.wait_ge(ff["y_out"], FC * u + c + 1)
                act.activation(act1[:, c, :], arg[:, c, :], ACT.Relu).then_inc(ff["relu"], 1)

            def feed_forward(u, before=True, now=True, following=True, more=True):
                for c in range(FC):
                    if now:
                        hidden(u, c)
                    if c == 1 and following:
                        ff_prepare(u + 1, 1)
                    if c == 1 and more:
                        ff_prepare(u + 2, 0)
                    if c and now:
                        sines(u, c - 1)
                    if c == 0 and before:
                        sines(u - 1, FC - 1)
                    if c >= 2 and now:
                        relu(u, c - 2)
                    if c < 2 and before:
                        relu(u - 1, c + 2)

            for stage in range(2):
                ff_prepare(0, stage)
            ff_prepare(1, 0)
            feed_forward(0, before=False)
            with act.Fori(0, NG - 3) as v:
                feed_forward(v + 1)
            feed_forward(NG - 2, more=False)
            feed_forward(NG - 1, following=False, more=False)
            feed_forward(NG, now=False, following=False, more=False)

        @block.vector
        def _(dve):
            own = Chain(dve, vec)
            dve.sem_inc(moe["mul"], 2)
            dve.memset(ps[:, PV_BANK, :], 0.0).then_inc(consts, 1)
            dve.sem_inc(moe["acc"], 2)
            for l in range(2):
                dve.sem_inc(s[l]["pv_done"], 2)

            def reduce_angle(dst, src):
                own.done(dve.tensor_scalar(tc1[:, :], src, 1.0 / TWO_PI, ROUND, ALU.mult, ALU.add))
                own.done(dve.tensor_scalar(tc1[:, :], tc1[:, :], ROUND, None, ALU.subtract))
                own.done(dve.scalar_tensor_tensor(tc2[:, :], tc1[:, :], -C1, src, ALU.mult, ALU.add))
                own.done(dve.scalar_tensor_tensor(tc2[:, :], tc1[:, :], -C2, tc2[:, :], ALU.mult, ALU.add))
                own.done(dve.tensor_scalar(dst, tc2[:, :], PI_IN, -PI_IN, ALU.min, ALU.max))

            dve.wait_ge(w_in, 16 * len(weights))
            reduce_angle(thr[:, :], th[:, :])
            own.done(dve.tensor_scalar(thc[:, :], thr[:, :], float(np.pi / 2), None, ALU.add))
            own.done(dve.scalar_tensor_tensor(argb[:, :], b1c[:, :], 0.1, thr[:, :], ALU.mult, ALU.add))
            own.done(dve.tensor_scalar(argb[:, :], argb[:, :], 1.0 / TWO_PI, None, ALU.mult))
            reduce_angle(thc[:, :], thc[:, :])
            dve.tensor_copy(thc[:, :], thc[:, :]).then_inc(theta["reduced"], 1)
            dve.wait_ge(theta["sines"], 2)
            own.done(dve.tensor_tensor(cos_th[:, :], cos_th[:, :], wrl[:, :], ALU.mult))
            own.done(dve.tensor_tensor(sin_th[:, :], sin_th[:, :], wim[:, :], ALU.mult))
            own.done(dve.tensor_tensor(cos_th[:, :], cos_th[:, :], sin_th[:, :], ALU.add))
            own.done(dve.scalar_tensor_tensor(coef[:, :], cos_th[:, :], 0.1, wim[:, :], ALU.mult, ALU.mult))

            CH_STATS = 4

            def statistics(u, ready):
                apart(dve)
                for k in range(GT):
                    last = dve.bn_stats(stats[:, k, :], x[:, u * GT + k, :])
                own.done(last)
                apart(dve)
                for k in range(GT):
                    last = dve.bn_aggr(mv[:, k, :], stats[:, k, :])
                last.then_inc(ready, 1)

            def normalise(u, rstd_ready, dst, done):
                dve.wait_ge(rstd_ready, u + 1)
                for k in range(GT):
                    last = dve.tensor_scalar(dst[:, k, :], x[:, u * GT + k, :], mv[:, k, 0:1], rstd[:, k:k + 1],
                                             ALU.subtract, ALU.mult)
                last.then_inc(done, 1)

            def project(l):
                sl = s[l]

                def norm(u):
                    statistics(u, sl["stats_ready"])
                    dve.wait_ge(sl["stats_ready"], u + 1)
                    dve.wait_ge(sl["turned"], u)
                    normalise(u, sl["rstd_ready"], tokens, sl["normed"])

                def split(u, half):
                    rows = (P, P if l == 0 else KV * HD)
                    if l == 1:
                        for n, out_sem in enumerate(("q_out", "k_out")):
                            dve.wait_ge(sl[out_sem], u + 1)
                            r = rows[n]
                            dve.wait_ge(sl["split_done"], 2 * u + AT_ONE)
                            dve.tensor_tensor(qk32[0:r, n, :], ps[0:r, 1 + n, :], ropeT[0:r, half * GW:(half + 1) * GW], ALU.mult)\
                                .then_inc(sl["qk_sb"], 1)
                    dve.wait_ge(sl["parts_written"], 32 * u + AT_ONE)
                    for n in range(2):
                        r = rows[n]
                        dve.wait_ge(sl["qk_sb"], 2 * u + n + 1 + AT_ONE)
                        a, z, pt = qk32[0:r, n, :], rest[0:r, n, :], parts[0:r, n]
                        own.done(dve.tensor_copy(pt[:, 0, :], a))
                        own.done(dve.tensor_tensor(z, a, pt[:, 0, :], ALU.subtract))
                        own.done(dve.tensor_copy(pt[:, 1, :], z))
                        dve.tensor_tensor(pt[:, 2, :], z, pt[:, 1, :], ALU.subtract).then_inc(sl["split_done"], 1)

                norm(0)
                per = 2 * 7
                with dve.Fori(0, NG // 2 - 1) as v:
                    own.loop(v, per)
                    for half in range(2):
                        norm(2 * v + half + 1)
                        split(2 * v + half, half)
                own.end_loop(NG // 2 - 1, per)
                norm(NG - 1)
                split(NG - 2, 0)
                split(NG - 1, 1)

            def attention(l):
                sl, hd = s[l], LAYERS[l]

                def row_max(quad, j, i, par):
                    n = 32 * quad + 8 * j + i
                    dve.wait_ge(sl["scores"], n + 1)
                    dve.tensor_reduce(rowmax[:, par, 8 * j + i:8 * j + i + 1], score_a(i % 2)[:, 0:hd.keys(i)],
                                      AX, ALU.max).then_inc(sl["max_done"], 1)

                def negmax_split(g, par):
                    dve.wait_ge(sl["max_done"], 32 * g + 32)
                    if not isinstance(g, int) or g > 0:
                        dve.wait_ge(sl["negmaxT_psum"], g)
                    mx = rowmax[:, par, :]
                    own.done(dve.tensor_scalar(negmax[:, 0, :], mx, -1.0, None, ALU.mult))
                    own.done(dve.scalar_tensor_tensor(negrest[:, :], mx, -1.0, negmax[:, 0, :],
                                                      ALU.mult, ALU.subtract))
                    own.done(dve.tensor_copy(negmax[:, 1, :], negrest[:, :]))
                    dve.tensor_tensor(negmax[:, 2, :], negrest[:, :], negmax[:, 1, :], ALU.subtract)\
                        .then_inc(sl["negmax_ready"], 1)

                def normalise_out(g, b, q, h):
                    dve.wait_ge(sl["o_turned"], 2 * g + h + 1 + AT_ONE)
                    o = ps[:, MISC, :].rearrange("p (k j c) -> p k j c", k=4, c=32)
                    own.done(dve.reciprocal(rden[:, :, :], o[:, :, :, HD]))
                    dst = attn[:, bass.ds(8 * b + 4 * h, 4), :]
                    dst = dst.rearrange("p k (a c i) -> p k a c i", a=4, c=4)
                    dst = dst[:, :, q, :, :] if l == 0 else dst[:, :, :, q, :]
                    dve.tensor_tensor(dst, o[:, :, :, 0:HD], rden[:, :, :].unsqueeze(3).broadcast_to([P, 4, 4, HD]),
                                      ALU.mult).then_inc(sl["attn_done"], 1)

                for n in range(32):
                    row_max(0, n // 8, n % 8, 0)
                for n in range(8):
                    row_max(1, 0, n, 1)
                negmax_split(0, 0)

                def batch(b, final):
                    for q in range(4):
                        g = 4 * b + q
                        more_1, more_2 = not (final and q == 3), not (final and q >= 2)
                        for ev in hd.events:
                            if ev[0] == "A":
                                k = ev[1]
                                if k < 24 and more_1:
                                    row_max(g + 1, 1 + k // 8, k % 8, (q + 1) % 2)
                                if k >= 24 and more_2:
                                    row_max(g + 2, 0, k % 8, q % 2)
                                if k == 23 and more_1:
                                    negmax_split(g + 1, (q + 1) % 2)
                            elif ev[0] == "ON":
                                normalise_out(g, b, q, ev[1])

                per = 4 * (3 + 2)
                with dve.Fori(0, B - 1) as b:
                    own.loop(b, per)
                    batch(b, False)
                own.end_loop(B - 1, per)
                batch(B - 1, True)

            def prepare(u, stage):
                if stage == 0:
                    dve.tensor_copy(tokens[:, :, :], attn[:, bass.ts(u, GT), :]).then_inc(pre["attn_staged"], 1)
                elif stage == 1:
                    dve.wait_ge(pre["wo_out"], u + 1)
                    xs = x[:, bass.ts(u, GT), :]
                    own.done(dve.tensor_tensor(xs, xs, ps[:, 7, :].rearrange("p (t d) -> p t d", t=GT), ALU.add))
                    statistics(u, pre["stats"])
                    dve.wait_ge(pre["stats"], u + 1)
                    normalise(u, pre["rstd"], tokens2, pre["normed"])
                elif stage == 3:
                    dve.wait_ge(pre["logits"], u + 1)
                    lg = ps[:, 7, 0:GT * E].rearrange("p (t e) -> p t e", t=GT)

                    def over_e(a):
                        return a.unsqueeze(2).broadcast_to([P, GT, E])

                    own.done(dve.tensor_reduce(r1[:, :], lg, AX, ALU.max))
                    dve.tensor_tensor(ra[:, :, :], lg, over_e(r1[:, :]), ALU.subtract).then_inc(pre["shifted"], 1)
                    dve.wait_ge(pre["exped"], u + 1)
                    own.done(dve.tensor_reduce(r1[:, :], rb[:, :, :], AX, ALU.add))
                    own.done(dve.reciprocal(r2[:, :], r1[:, :]))
                    own.done(dve.tensor_tensor(rb[:, :, :], rb[:, :, :], over_e(r2[:, :]), ALU.mult))
                    mine = rb[:, :, :].unsqueeze(3).broadcast_to([P, GT, E, E])
                    other = rb[:, :, :].unsqueeze(2).broadcast_to([P, GT, E, E])
                    dve.tensor_tensor(cmp1[:, :, :, :], other, mine, ALU.is_gt)
                    own.done(dve.tensor_tensor(cmp2[:, :, :, :], other, mine, ALU.is_equal))
                    own.done(dve.tensor_tensor(cmp2[:, :, :, :], cmp2[:, :, :, :],
                                               lower[:, :, :].unsqueeze(1).broadcast_to([P, GT, E, E]), ALU.mult))
                    own.done(dve.tensor_tensor(cmp1[:, :, :, :], cmp1[:, :, :, :], cmp2[:, :, :, :], ALU.add))
                    own.done(dve.tensor_reduce(ra[:, :, :], cmp1[:, :, :, :], AX, ALU.add))
                    own.done(dve.scalar_tensor_tensor(rc[:, :, :], ra[:, :, :], 2.0, rb[:, :, :],
                                                      ALU.is_lt, ALU.mult))
                    own.done(dve.tensor_reduce(r1[:, :], rc[:, :, :], AX, ALU.add))
                    own.done(dve.reciprocal(r2[:, :], r1[:, :]))
                    dve.tensor_tensor(ew[:, bass.ts(u, GT), :], rc[:, :, :], over_e(r2[:, :]), ALU.mult)\
                        .then_inc(pre["weights"], 1)

            def multiply(u, e):
                for c, (f, w) in enumerate(FCH):
                    n = 3 * (E * u + e) + c
                    par = (3 * e + c) % 2
                    if c == 0 and e:
                        dve.wait_ge(moe["down"], E * u + e - 1 + AT_ONE)
                    dve.wait_ge(moe["silu"], n + 3)
                    dve.wait_ge(moe["up"], n + 1)
                    dve.tensor_tensor(acts[0:w, e % 2, c, :], ps[0:w, 2 + par, :], gated[0:w, par, :], ALU.mult)\
                        .then_inc(moe["mul"], 1)

            def accumulate(u, e):
                n = E * u + e
                dve.wait_ge(moe["down"], n + 1 + AT_ONE)
                dve.wait_ge(moe["acc"], n + 2)
                if e == 0:
                    dve.wait_ge(pre["weights"], u + 1)
                for k in range(GT):
                    xs = x[:, u * GT + k, :]
                    last = dve.scalar_tensor_tensor(xs, ps[:, 4 + e % 2, k * D:(k + 1) * D],
                                                    ew[:, u * GT + k, e:e + 1], xs, ALU.mult, ALU.add)
                last.then_inc(moe["acc"], 1)

            def experts(u, more):
                for e in range(E):
                    multiply(u, e)
                    if e:
                        accumulate(u, e - 1)
                    if more and e in (0, 3):
                        prepare(u + 1, e // 2)
                accumulate(u, E - 1)
                if more:
                    prepare(u + 1, 3)

            dve.wait_ge(x_in, 16)
            project(0)
            attention(0)
            dve.wait_ge(s[0]["attn_done"], 2 * NQ + AT_ONE)
            for stage in range(4):
                prepare(0, stage)
            chain = 2 + 11
            with dve.Fori(0, NG - 1) as u:
                own.loop(u, chain)
                experts(u, True)
            own.end_loop(NG - 1, chain)
            experts(NG - 1, False)
            dve.wait_ge(moe["acc"], E * NG + 2)
            project(1)
            attention(1)
            dve.wait_ge(s[1]["attn_done"], 2 * NQ + AT_ONE)

            def ff_prepare(u, stage):
                if stage == 0:
                    dve.wait_ge(ff["a_turned"], u + AT_ONE)
                    dve.tensor_copy(tokens[:, :, :], attn[:, bass.ts(u, GT), :]).then_inc(ff["attn_staged"], 1)
                elif stage == 1:
                    xs = x[:, bass.ts(u, GT), :]
                    dve.wait_ge(ff["wo_out"], u + 1)
                    own.done(dve.tensor_tensor(xs, xs, ps[:, 1, :].rearrange("p (t d) -> p t d", t=GT), ALU.add))
                    statistics(u, ff["stats"])
                else:
                    dve.wait_ge(ff["stats"], u + 1)
                    if not isinstance(u, int) or u > 0:
                        dve.wait_ge(ff["turned"], u)
                    normalise(u, ff["rstd"], tokens2, ff["normed"])

            def reduced(u, c):
                dve.wait_ge(ff["turns"], FC * u + c + 1)
                dve.tensor_tensor(arg[:, c, :], arg[:, c, :], turns[:, c, :], ALU.subtract)\
                    .then_inc(ff["reduced"], 1)

            def mixed(u, c):
                dve.wait_ge(ff["sine"], FC * u + c + 1)
                a = arg[:, c, :]
                dve.scalar_tensor_tensor(a, a, coef[:, c:c + 1], hid[:, c, :], ALU.mult, ALU.add)\
                    .then_inc(ff["mixed"], 1)

            def finish(u):
                dve.wait_ge(ff["y_out"], FC * u + 2 * FC)
                dve.wait_ge(ff["added"], u + 1)
                dve.tensor_tensor(y[:, :, :], y[:, :, :], ps[:, 6, :].rearrange("p (t d) -> p t d", t=GT),
                                  ALU.add).then_inc(ff["y_ready"], 1)

            def feed_forward(u, before=True, now=True, following=True, more=True):
                for c in range(FC):
                    if c and now:
                        reduced(u, c - 1)
                    if c == 0 and before:
                        reduced(u - 1, FC - 1)
                    if c >= 2 and now:
                        mixed(u, c - 2)
                    if c < 2 and before:
                        mixed(u - 1, c + 2)
                    if c in (0, 1, 3) and more:
                        ff_prepare(u + 2, min(c, 2))
                    if c == 2 and before:
                        finish(u - 1)

            for stage in range(3):
                ff_prepare(0, stage)
            for stage in range(3):
                ff_prepare(1, stage)
            feed_forward(0, before=False)
            with dve.Fori(0, NG - 3) as v:
                own.loop(v, 2)
                feed_forward(v + 1)
            own.end_loop(NG - 3, 2)
            feed_forward(NG - 2, more=False)
            feed_forward(NG - 1, following=False, more=False)
            feed_forward(NG, now=False, following=False, more=False)


_INS = ["L0_attn_h", "L0_attn_Wqvk", "L0_attn_Wo", "L0_ffn_router_w", "L0_ffn_gate_proj", "L0_ffn_up_proj",
        "L0_ffn_down_proj", "L1_attn_w_q", "L1_attn_w_k", "L1_attn_w_v", "L1_attn_w_o", "L1_attn_g", "L1_ffn_W1",
        "L1_ffn_b1", "L1_ffn_quantum_phases", "L1_ffn_quantum_weights_real", "L1_ffn_quantum_weights_imag",
        "L1_ffn_W2", "L1_ffn_b2"]


def rope_table():
    i = np.arange(HD)
    theta = np.power(np.float32(10000.0), (-2.0 * (i // 2) / HD).astype(np.float32))
    angle = np.arange(S, dtype=np.float32)[:, None] * theta[None, :]
    sign = np.where(np.arange(S) % 2 == 1, -1.0, 1.0).astype(np.float32)
    factor = np.cos(angle) + sign[:, None] * np.sin(angle)
    return np.ascontiguousarray(np.tile(factor.T, (H, 1)), dtype=np.float32)


_COLUMNS = {"L1_attn_g", "L1_ffn_b1", "L1_ffn_quantum_phases", "L1_ffn_quantum_weights_real",
            "L1_ffn_quantum_weights_imag"}


def kernel(**inputs):
    import concourse.bacc as bacc
    from concourse.bass_utils import run_bass_kernel_spmd

    nc = bacc.Bacc("TRN2", target_bir_lowering=False, num_devices=1)
    arrays, args = {}, []
    for name, a in [(n, inputs[n]) for n in _INS] + [("rope", rope_table())]:
        a = np.asarray(a)
        a = np.ascontiguousarray(a.reshape(-1, P).T if name in _COLUMNS else a)
        arrays[f"in_{name}_dram"] = a
        args.append(nc.dram_tensor(f"in_{name}_dram", a.shape, mybir.dt.from_np(a.dtype), kind="ExternalInput").ap())
    out = nc.dram_tensor("out_0_dram", (B, S, D), F32, kind="ExternalOutput").ap()
    build(nc, *args, out)
    r = run_bass_kernel_spmd(nc, [arrays], core_ids=[0])
    return r.results[0]["out_0_dram"]
```

```python
from contextlib import ExitStack

import numpy as np

import concourse.bass as bass
from concourse import mybir

F32 = mybir.dt.float32
BF16 = mybir.dt.bfloat16
ALU = mybir.AluOpType
ACT = mybir.ActivationFunctionType
AX = mybir.AxisListType.X

P = 128
B, S, D = 4, 1024, 128
H, HD, KV = 16, 8, 4
T = B * S // P
GT = 4
NG = T // GT
GW = GT * P
E, F0 = 8, 352
FCH = [(0, 128), (128, 128), (256, 96)]
F1 = 512
FC = F1 // P
LN_EPS = 1e-5
RMS_EPS = float(np.finfo(np.float32).eps)
SCALE = 1.0 / float(np.sqrt(D))
MASKED = -1e30

NQ = B * 4
SPL = 3
CROSS = SPL * SPL * HD
KROWS = CROSS + SPL
SLOTS = 4
PR = 8
HALF = 512

TWO_PI = 2.0 * np.pi
C1 = 6.28125
C2 = float(TWO_PI - C1)
ROUND = 12582912.0
PI_IN = 3.1415925


TWO_ONES = float(np.uint32(0x3F803F80).view(np.float32))
AT_ONE = 1


class Chain:

    def __init__(self, eng, sem, own_wait=False):
        self.eng, self.sem, self.start, self.n, self.own_wait = eng, sem, 0, 0, own_wait

    def done(self, ins):
        self.n += 1
        ins.then_inc(self.sem, 1)
        self.eng.wait_ge(self.sem, self.start + self.n)
        if self.own_wait:
            self.eng.nop(nofuse=True)

    def loop(self, turn, each):
        self.first = self.start + self.n
        self.start, self.n = self.first + turn * each, 0

    def end_loop(self, turns, each):
        assert self.n == each, (self.n, each)
        self.start, self.n = self.first + turns * each, 0


class Heads:

    def __init__(self, causal, letters):
        self.causal = causal
        self.groups = [(h, t) for h in range(2) for t in range(8) if not causal or t // 4 <= h]
        self.G = len(self.groups)
        self.last_of_half = [max(m for m, (h, _) in enumerate(self.groups) if h == half) for half in range(2)]
        self.events = self.order(letters)

    def cols(self, m):
        h, t = self.groups[m]
        return max(0, P * t - HALF * h) if self.causal else 0

    def diagonal(self, m):
        h, t = self.groups[m]
        return self.causal and t // 4 == h

    def keys(self, i):
        return P * (i + 1) if self.causal else S

    def order(self, letters):
        out, count, borrowed = [], dict.fromkeys("abpmsctn", 0), []
        for at, letter in enumerate(letters):
            n = count[letter]
            count[letter] += 1
            if letter == "b":
                out.append(("B", n // 4, n % 4))
            elif letter == "a":
                out.append(("A", n))
            elif letter == "p":
                out.append(("PV", n))
            elif letter == "c":
                out.append(("OC", n))
            elif letter in "mt":
                reader = letters.index("n" if letter == "t" else "s", at)
                unit = count["a"] + letters[at:reader].count("a")
                assert unit - count["a"] <= 1
                borrowed.append((unit, "MC" if letter == "m" else "ON", n))
                out.append(("MT", n, unit, count["n"]) if letter == "m" else ("OT", n, unit, count["s"]))
            else:
                kind = {"n": "ON", "s": "MC"}[letter]
                out.append((kind, n, next(u for u, k, h in borrowed if (k, h) == (kind, n))))
        assert list(count.values()) == [32, 4 * self.G, self.G, 1, 1, 2, 2, 2]
        self.readers = {u: [(k, h) for v, k, h in borrowed if v == u] for u in range(33)}
        return out


ORDERS = [
    "bbbbaabpaabbbabapabbbabbpbbbabapcabbbatbpnbababbabbapapaabbababbababbapbbbaabpbampsabbabbabbbappactn",
    "bbbbababbpbabbapbbababbpbabbabpbbababbpabbapbbababbpbbbapcabbtnbpbabbabbapbabbabbapabbbabpbbbababpmsbbbabapbabbbapapactn",
]
EARLY = {
    "tensor": [{1: (0, 0), 3: (0, 1), 6: (0, 2), 8: (0, 3)},
               {1: (0, 0), 3: (0, 1), 6: (0, 2), 7: (1, 0), 9: (1, 1)}],
    "vector": [{0: (0, 0), 3: (0, 1), 5: (0, 2), 8: (0, 3)},
               {0: (0, 0), 3: (0, 1), 5: (0, 2), 6: (1, 0), 9: (1, 1), 11: (1, 2)}],
    "scalar": [{2: (0, 0), 7: (0, 2), 9: (0, 3)}, {2: (0, 0), 7: (0, 1), 8: (1, 0)}],
}
LAYERS = [Heads(True, ORDERS[0]), Heads(False, ORDERS[1])]
QUAD_LOADS = 2 * SPL * SPL + 1


def build(nc, h_in, Wqvk, Wo0, router_w, gate_proj, up_proj, down_proj, w_q, w_k, w_v, w_o, g_rms,
          W1, b1, phases, w_real, w_imag, W2, b2, rope, out):
    q_parts = [nc.dram_tensor(f"q_parts{l}", (SPL, P, B * S), BF16, kind="Internal").ap() for l in range(2)]
    k_parts = [nc.dram_tensor(f"k_parts{l}", (SPL, r, B * S), BF16, kind="Internal").ap()
               for l, r in enumerate((P, KV * HD))]
    x_dram = h_in.rearrange("b (t p) d -> p (b t) d", p=P)
    out_dram = out.rearrange("b (t p) d -> p (b t) d", p=P)

    with ExitStack() as ctx:
        def sb(name, shape, dt=F32):
            return ctx.enter_context(nc.sbuf_tensor(name, shape, dt))

        def sem(name):
            return ctx.enter_context(nc.semaphore(name))

        x = sb("x", [P, T, D])
        attn = sb("attn", [P, T, D])
        v1 = sb("v1", [P, T, H * (HD + 1)])
        Q = sb("Q", [P, SLOTS, 4, S], BF16)
        K = sb("K", [P, SLOTS, 4, S], BF16)
        V = sb("V", [P, SLOTS, 8, 4 * (HD + 1)])
        probs = sb("probs", [P, PR, HALF])
        oT = sb("oT", [P, HALF])
        rowmax = sb("rowmax", [P, 2, 32])
        negmax = sb("negmax", [P, SPL, 32], BF16)
        negrest = sb("negrest", [P, 32])
        negmaxT = sb("negmaxT", [SPL * 32, P], BF16)
        rden = sb("rden", [P, 4, 4])
        spare = Q[:, :, :, :].rearrange("p s j n -> p (s j n)").bitcast(F32)
        hT_all = spare[:, 0:B * S]
        acts = spare[:, B * S:B * S + 6 * GW].rearrange("p (a c n) -> p a c n", a=2, c=len(FCH))
        gated = spare[:, B * S + 6 * GW:B * S + 8 * GW].rearrange("p (a n) -> p a n", a=2)
        act1 = spare[:, B * S:B * S + FC * GW].rearrange("p (c n) -> p c n", c=FC)
        spare_k = K[:, :, :, :].rearrange("p s j n -> p (s j n)").bitcast(F32)
        hid, arg, turns = (spare_k[:, n * FC * GW:(n + 1) * FC * GW].rearrange("p (c n) -> p c n", c=FC)
                           for n in range(3))
        ident = sb("ident", [P, P])
        identb = sb("identb", [P, P], BF16)
        causal = sb("causal", [P, P], BF16)
        wqvk = sb("wqvk", [P, 3 * D])
        wo0 = sb("wo0", [P, D])
        wr = sb("wr", [P, E])
        wg = sb("wg", [P, E, F0])
        wu = sb("wu", [P, E, F0])
        wd = sb("wd", [P, len(FCH), E, D])
        wq1 = sb("wq1", [P, D])
        wk1 = sb("wk1", [P, KV * HD])
        wv1 = sb("wv1", [P, KV * HD])
        wo1 = sb("wo1", [P, D])
        gcol = sb("gcol", [P, 1])
        w1 = sb("w1", [P, F1])
        w2 = sb("w2", [P, FC, D])
        b1c = sb("b1c", [P, FC])
        th = sb("th", [P, FC])
        wrl = sb("wrl", [P, FC])
        wim = sb("wim", [P, FC])
        b2r = sb("b2r", [P, D])
        ropeT = sb("ropeT", [P, S])
        BT = T // B
        stats_b = sb("stats_b", [P, BT, 6])
        mv_all = sb("mv_all", [P, T, 2])
        rstd_all = sb("rstd_all", [P, T])
        rtmp_b = sb("rtmp_b", [P, T])
        power_b = sb("power_b", [P, T // B])
        mv1 = sb("mv1", [P, GT, 2])
        rms = sb("rms", [P, GT])
        rtmp1 = sb("rtmp1", [P, GT])
        stats = sb("stats", [P, GT, 6])
        mv = sb("mv", [P, GT, 2])
        rstd = sb("rstd", [P, GT])
        rtmp = sb("rtmp", [P, GT])
        power = sb("power", [P, GT])
        tokens = sb("tokens", [P, GT, D])
        tokens2 = sb("tokens2", [P, GT, D])
        hT = sb("hT", [P, GW])
        aT = sb("aT", [P, GW])
        qk32 = probs[:, 0:2, :]
        rest = probs[:, 2:4, :]
        parts = spare[:, B * S:B * S + 2 * SPL * GW].bitcast(BF16)\
            .rearrange("p (two a c n) -> p two a c n", two=2, a=2, c=SPL)
        ew = sb("ew", [P, T, E])
        lower = sb("lower", [P, E, E])
        ra = sb("ra", [P, GT, E])
        rb = sb("rb", [P, GT, E])
        rc = sb("rc", [P, GT, E])
        r1 = sb("r1", [P, GT])
        r2 = sb("r2", [P, GT])
        cmp1 = sb("cmp1", [P, GT, E, E])
        cmp2 = sb("cmp2", [P, GT, E, E])
        tc1 = sb("tc1", [P, FC])
        tc2 = sb("tc2", [P, FC])
        thr = sb("thr", [P, FC])
        thc = sb("thc", [P, FC])
        sin_th = sb("sin_th", [P, FC])
        cos_th = sb("cos_th", [P, FC])
        coef = sb("coef", [P, FC])
        argb = sb("argb", [P, FC])
        y = sb("y", [P, GT, D])

        ps = ctx.enter_context(nc.psum_tensor("ps", [P, 8, 512], F32))
        def score_a(n):
            return ps[:, 2 * n:2 * n + 2, :].rearrange("p b n -> p (b n)")

        def turn_bank(unit):
            return 2 * (unit % 2)

        PV_BANK, B_BANKS = 6, (4, 5, 7)

        x_in = [sem(f"x_in{b}") for b in range(B)]
        wqvk_in, w_in = sem("wqvk_in"), sem("w_in")
        consts, k_ones = sem("consts"), sem("k_ones")
        rstd_first = sem("rstd_first")
        vec, pool_own = sem("vector_own"), sem("gpsimd_own")
        names = ("normed", "turned", "h_ready", "stats_ready", "rstd_ready", "q_out", "k_out", "v_out",
                 "qk_sb", "v_taken", "hi_done", "rest_done", "mid_done", "split_done", "scores", "max_done",
                 "negmax_ready", "negmaxT_psum", "negmaxT_ready", "negmax_rows", "scoresT", "exp_done", "pv_done",
                 "o_copied", "o_turned", "attn_done")
        from_one = ("rstd_ready", "qk_sb", "v_taken", "rest_done", "split_done", "o_copied", "o_turned",
                    "attn_done")
        s = [{n: sem(f"{n}{l}") for n in names} for l in range(2)]
        for l in range(2):
            s[l]["parts_written"] = [sem(f"parts_written{l}_{half}") for half in range(2)]
        loaded = [[sem(f"loaded{l}_{k}") for k in range(SLOTS)] for l in range(2)]
        pre = {n: sem("pre_" + n) for n in
               ("attn_staged", "a_turned", "a_ready", "wo_out", "stats", "rstd", "normed", "turned", "h_ready",
                "logits", "shifted", "exped", "ranked", "weights")}
        moe = {n: sem("moe_" + n) for n in ("gate", "up", "silu", "mul", "down", "acc")}
        ff = {n: sem("ff_" + n) for n in
              ("attn_staged", "a_turned", "a_ready", "wo_out", "added", "stats", "rstd", "normed", "turned", "h_ready",
               "hidden", "arg", "hid", "turns", "reduced", "sine", "mixed", "relu", "y_out", "y_ready", "stored")}
        theta = {n: sem("theta_" + n) for n in ("reduced", "sines")}

        weights = [
            (wo0[:, :], Wo0), (wr[:, :], router_w),
            (wg[:, :, :], gate_proj.rearrange("e d f -> d e f")), (wu[:, :, :], up_proj.rearrange("e d f -> d e f")),
            *[(wd[0:w, c, :, :], down_proj[:, f:f + w, :].rearrange("e f d -> f e d")) for c, (f, w) in enumerate(FCH)],
            (wq1[:, :], w_q), (wk1[:, :], w_k), (wv1[:, :], w_v), (wo1[:, :], w_o), (gcol[:, :], g_rms),
            (w1[:, :], W1), (w2[:, :, :], W2.rearrange("(c p) d -> p c d", p=P)), (b1c[:, :], b1),
            (th[:, :], phases), (wrl[:, :], w_real), (wim[:, :], w_imag),
            (b2r[:, :], b2.rearrange("(a d) -> a d", a=1).broadcast_to([P, D])), (ropeT[:, :], rope),
        ]

        starting = [s[l][n] for l in range(2) for n in from_one] + [moe["down"]] + \
            [ff[n] for n in ("arg", "y_ready", "a_turned", "stored")]

        block = ctx.enter_context(nc.Block())

        def ones_rows(a, b):
            return K[64:96, a:b, :, :].rearrange("p s j n -> p (s j n)").bitcast(F32)

        def apart(eng):
            eng.nop(nofuse=True)

        @block.sync
        def _(sp):
            for b in range(B):
                tiles = slice(b * BT, (b + 1) * BT)
                sp.dma_start(x[:, tiles, :], x_dram[:, tiles, :]).then_inc(x_in[b], 16)
            for semaphore in starting:
                sp.sem_inc(semaphore, 1)
            sp.sem_inc(ff["y_out"], FC)
            for l in range(2):
                sl = s[l]

                def load(b, q):
                    for a in range(SPL):
                        heads = q_parts[l][a, :, bass.ts(b, S)].rearrange("(h i) n -> i h n", i=HD)
                        heads = heads[:, 4 * q:4 * q + 4, :] if l == 0 else heads[:, q:H:KV, :]
                        for r in range(SPL):
                            row = (a * SPL + r) * HD
                            sp.dma_start(Q[row:row + HD, q, :, :], heads).then_inc(loaded[l][q], 16)
                            keys = k_parts[l][r, :, bass.ts(b, S)].rearrange("(h i) n -> i h n", i=HD)
                            keys = keys[:, 4 * q:4 * q + 4, :] if l == 0 else keys[:, q:q + 1, :]
                            sp.dma_start(K[row:row + HD, q, 0:keys.shape[1], :], keys).then_inc(loaded[l][q], 16)
                    w = (HD + 1) * (4 if l == 0 else 1)
                    sp.dma_start(V[:, q, :, 0:w], v1[:, bass.ts(b, 8), w * q:w * q + w]).then_inc(loaded[l][q], 16)

                def negmax_rows(q, g):
                    sp.wait_ge(sl["negmaxT_ready"], g + 1)
                    sp.dma_start(Q[CROSS:KROWS, q, :, :].rearrange("c j (i n) -> c (j i) n", n=P),
                                 negmaxT[:, :]).then_inc(sl["negmax_rows"], 16)

                sp.wait_ge(k_ones, 2)
                sp.wait_ge(sl["v_taken"], 2 + AT_ONE)
                for half in range(2):
                    sp.wait_ge(sl["parts_written"][half], 32)
                for q in range(2):
                    load(0, q)
                sp.wait_ge(sl["v_taken"], NG + AT_ONE)
                for half in range(2):
                    sp.wait_ge(sl["parts_written"][half], 32 * (NG // 2))
                load(0, 2)
                negmax_rows(0, 0)

                def batch(b, final):
                    for q in range(4):
                        g = 4 * b + q
                        if q == 0 or not final:
                            sp.wait_ge(sl["o_turned"], 2 * g + AT_ONE)
                            load(b if q == 0 else b + 1, (q + 3) % 4)
                        if q < 3 or not final:
                            negmax_rows((q + 1) % 4, g + 1)

                with sp.Fori(0, B - 1) as b:
                    batch(b, False)
                batch(B - 1, True)

            with sp.Fori(0, NG) as u:
                sp.wait_ge(ff["y_ready"], u + 1 + AT_ONE)
                sp.dma_start(out_dram[:, bass.ts(u, GT), :], y[:, :, :]).then_inc(ff["stored"], 16)
            sp.wait_ge(ff["stored"], 16 * NG + AT_ONE)

        @block.gpsimd
        def _(pool):
            own = Chain(pool, pool_own, own_wait=True)
            own.done(pool.memset(ident[:, :], 0.0))
            own.done(pool.memset(identb[:, :], 0.0))
            own.done(pool.memset(causal[:, :], 0.0))
            own.done(pool.memset(lower[:, :, :], 0.0))
            own.done(pool.memset(power[:, :], -0.5))
            own.done(pool.memset(power_b[:, :], -0.5))
            for m in (ident, identb):
                pool.affine_select(out=m[:, :], in_=m[:, :], compare_op=ALU.not_equal, fill=1.0, base=0,
                                   pattern=[[-1, P]], channel_multiplier=1).then_inc(consts, 1)
            pool.affine_select(out=causal[:, :], in_=causal[:, :], compare_op=ALU.is_ge, fill=MASKED, base=0,
                               pattern=[[-1, P]], channel_multiplier=1).then_inc(consts, 1)
            pool.affine_select(out=lower[:, :, :], in_=lower[:, :, :], compare_op=ALU.is_ge, fill=1.0, base=0,
                               pattern=[[-1, E], [1, E]], channel_multiplier=0).then_inc(consts, 1)
            pool.memset(v1[:, :, HD::HD + 1], 1.0).then_inc(consts, 1)
            pool.wait_ge(consts, 5)
            apart(pool)

            def inverse(ready, done, u):
                pool.wait_ge(ready, u + 1)
                apart(pool)
                own.done(pool.tensor_scalar(rtmp[:, :], mv[:, :, 1], LN_EPS, 1.0, ALU.add, ALU.mult))
                pool.tensor_tensor(rstd[:, :], rtmp[:, :], power[:, :], ALU.pow).then_inc(done, 1)

            def inverse_of_batches():
                for b in range(B):
                    pool.wait_ge(s[0]["stats_ready"], b + 1)
                    apart(pool)
                    tiles = slice(b * BT, (b + 1) * BT)
                    own.done(pool.tensor_scalar(rtmp_b[:, tiles], mv_all[:, tiles, 1], LN_EPS, 1.0, ALU.add, ALU.mult))
                    own.done(pool.tensor_tensor(rstd_all[:, tiles], rtmp_b[:, tiles], power_b[:, :], ALU.pow))
                    pool.sem_inc(rstd_first if b == 0 else s[0]["rstd_ready"], 1)

            def inverse_rms(u):
                pool.wait_ge(s[1]["stats_ready"], u + 1)
                apart(pool)
                var = mv1[:, :, 1]
                own.done(pool.tensor_scalar(rtmp1[:, :], var, LN_EPS, 1.0, ALU.add, ALU.mult))
                own.done(pool.tensor_tensor(rms[:, :], rtmp1[:, :], power[:, :], ALU.pow))
                own.done(pool.tensor_tensor(rtmp1[:, :], var, rms[:, :], ALU.mult))
                own.done(pool.tensor_tensor(rtmp1[:, :], rtmp1[:, :], rms[:, :], ALU.mult))
                own.done(pool.tensor_scalar(rtmp1[:, :], rtmp1[:, :], RMS_EPS, 1.0, ALU.add, ALU.mult))
                own.done(pool.tensor_tensor(rtmp1[:, :], rtmp1[:, :], power[:, :], ALU.pow))
                own.done(pool.tensor_tensor(rstd_all[:, bass.ts(u, GT)], rms[:, :], rtmp1[:, :], ALU.mult))
                pool.sem_inc(s[1]["rstd_ready"], 1)

            def write_parts(l):
                sl = s[l]
                rows_k = P if l == 0 else KV * HD
                with pool.Fori(0, NG // 2) as v:
                    for half in range(2):
                        u = 2 * v + half
                        pool.wait_ge(sl["split_done"], 2 * u + 2 + AT_ONE)
                        pool.dma_start(q_parts[l][:, :, bass.ts(u, GW)].rearrange("c p n -> p c n"),
                                       parts[:, half, 0, :, :]).then_inc(sl["parts_written"][half], 16)
                        pool.dma_start(k_parts[l][:, :, bass.ts(u, GW)].rearrange("c p n -> p c n"),
                                       parts[0:rows_k, half, 1, :, :]).then_inc(sl["parts_written"][half], 16)

            own.done(pool.memset(ones_rows(0, 2), TWO_ONES))
            pool.sem_inc(k_ones, 1)
            inverse_of_batches()
            write_parts(0)
            inverse(pre["stats"], pre["rstd"], 0)
            with pool.Fori(0, NG - 1) as u:
                own.loop(u, 8)
                inverse(pre["stats"], pre["rstd"], u + 1)
                inverse_rms(u)
            own.end_loop(NG - 1, 8)
            inverse_rms(NG - 1)
            write_parts(1)

            def turn_counts(u, c):
                pool.wait_ge(ff["arg"], FC * u + c + 1 + AT_ONE)
                apart(pool)
                own.done(pool.tensor_scalar(turns[:, c, :], arg[:, c, :], 1.0, ROUND, ALU.mult, ALU.add))
                pool.tensor_scalar(turns[:, c, :], turns[:, c, :], -ROUND, 1.0,
                                   ALU.add, ALU.mult).then_inc(ff["turns"], 1)

            def add_b2(u):
                pool.wait_ge(ff["stored"], 16 * u + AT_ONE)
                pool.tensor_tensor(y[:, :, :], x[:, bass.ts(u, GT), :],
                                   b2r[:, :].unsqueeze(1).broadcast_to([P, GT, D]), ALU.add)\
                    .then_inc(ff["added"], 1)

            def feed_forward(u, before=True, now=True, following=True, more=True):
                for c in range(FC):
                    if now:
                        turn_counts(u, c)
                    if c == 2 and more:
                        inverse(ff["stats"], ff["rstd"], u + 2)
                    if c == 1 and before:
                        add_b2(u - 1)

            inverse(ff["stats"], ff["rstd"], 0)
            inverse(ff["stats"], ff["rstd"], 1)
            feed_forward(0, before=False)
            with pool.Fori(0, NG - 3) as v:
                own.loop(v, 1 + FC)
                feed_forward(v + 1)
            own.end_loop(NG - 3, 1 + FC)
            feed_forward(NG - 2, more=False)
            feed_forward(NG - 1, following=False, more=False)
            feed_forward(NG, now=False, following=False, more=False)

        @block.tensor
        def _(pe):
            def turn(src, bank, done):
                for k in range(GT):
                    last = pe.transpose(ps[:, bank, k * P:(k + 1) * P], src[:, k, :], ident[:, :])
                last.then_inc(done, 1)

            def project(l):
                sl = s[l]
                if l == 0:
                    wq, wv, wk = (wqvk[:, n * D:(n + 1) * D] for n in range(3))
                    rk, wd_v = P, D
                else:
                    wq, wk, wv, rk, wd_v = wq1[:, :], wk1[:, :], wv1[:, :], KV * HD, KV * HD
                read = sl["rest_done"] if l == 0 else sl["qk_sb"]

                def turned(u, half):
                    pe.wait_ge(sl["normed"], u + 1)
                    turn(tokens, 4 * half, sl["turned"])

                def projected(u, half):
                    h, bank = (hT, aT)[half], 4 * half
                    pe.wait_ge(sl["h_ready"], u + 1)
                    if not isinstance(u, int) or u >= 2:
                        pe.wait_ge(read, 2 * u - 2 + AT_ONE)
                        pe.wait_ge(sl["v_taken"], u - 1 + AT_ONE)
                    pe.matmul(ps[:, bank + 1, :], wq, h[:, :], start=True, stop=True).then_inc(sl["q_out"], 1)
                    pe.matmul(ps[0:rk, bank + 2, :], wk, h[:, :], start=True, stop=True).then_inc(sl["k_out"], 1)
                    for k in range(GT):
                        last = pe.matmul(ps[:, bank + 3, k * wd_v:(k + 1) * wd_v], h[:, k * P:(k + 1) * P], wv,
                                         start=True, stop=True)
                    last.then_inc(sl["v_out"], 1)

                turned(0, 0)
                turned(1, 1)
                projected(0, 0)
                for half in range(2):
                    projected(half + 1, 1 - half)
                    turned(half + 2, half)
                with pe.Fori(0, NG // 2 - 2) as v:
                    for half in range(2):
                        projected(2 * v + half + 3, 1 - half)
                        turned(2 * v + half + 4, half)
                projected(NG - 1, 1)
                pe.wait_ge(read, 2 * NG - 2 + AT_ONE)
                pe.wait_ge(sl["v_taken"], NG - 1 + AT_ONE)

            def attention(l):
                sl, hd = s[l], LAYERS[l]
                G, nB = hd.G, 4 * hd.G
                rows = HD + 1

                def pass_a(quad, slot, j, i):
                    n = 32 * quad + 8 * j + i
                    buf = score_a(i % 2)
                    kj = j if l == 0 else 0
                    if not isinstance(n, int) or n >= 2:
                        pe.wait_ge(sl["max_done"], n - 1)
                    w = hd.keys(i)
                    for c in range(0, w, 512):
                        e = min(c + 512, w)
                        diag = hd.causal and e == w
                        last = pe.matmul(buf[:, c:e], Q[0:CROSS, slot, j, i * P:(i + 1) * P],
                                         K[0:CROSS, slot, kj, c:e], start=True, stop=not diag)
                        if diag:
                            last = pe.matmul(buf[:, w - P:w], identb[:, :], causal[:, :],
                                             start=False, stop=True)
                    last.then_inc(sl["scores"], 1)

                def borrowed(k, g):
                    for kind, h in hd.readers[k]:
                        if kind == "ON":
                            pe.wait_ge(sl["attn_done"], 2 * g + h + 1 + AT_ONE)
                        else:
                            pe.wait_ge(sl["negmaxT_ready"], g + 2)

                def free(k, g):
                    n = 32 * (g + 1) + 8 + k
                    if isinstance(g, int):
                        n = min(n, 32 * NQ + 1)
                    pe.wait_ge(sl["max_done"], n - 1)

                def pass_b(g, q, m, j):
                    i = 4 * m + j
                    n = nB * g + i
                    h, t = hd.groups[m]
                    c = hd.cols(m)
                    bank = B_BANKS[i % 3]
                    pe.wait_ge(sl["exp_done"], n + 1 if i or nB % 3 == 0 else n + 3)
                    kj = j if l == 0 else 0
                    diag = hd.diagonal(m)
                    last = pe.matmul(ps[:, bank, c:HALF], K[0:KROWS, q, kj, t * P:(t + 1) * P],
                                     Q[0:KROWS, q, j, h * HALF + c:(h + 1) * HALF], start=True, stop=not diag)
                    if diag:
                        last = pe.matmul(ps[:, bank, c:c + P], causal[:, :], identb[:, :],
                                         start=False, stop=True)
                    last.then_inc(sl["scoresT"], 1)

                def pv(g, q, m):
                    h, t = hd.groups[m]
                    c = hd.cols(m)
                    if t == 0:
                        pe.wait_ge(sl["o_copied"], 2 * g + h + AT_ONE)
                    for j in range(4):
                        n = nB * g + 4 * m + j
                        pe.wait_ge(sl["exp_done"], n + 4)
                        kj = j if l == 0 else 0
                        last = pe.matmul(ps[32 * j:32 * j + rows, PV_BANK, c:HALF],
                                         V[:, q, t, kj * rows:(kj + 1) * rows],
                                         probs[:, (4 * m + j) % PR, c:HALF],
                                         start=(t == 0), stop=(m == hd.last_of_half[h]), skip_group_check=True)
                    last.then_inc(sl["pv_done"], 1)

                def negmax_turn(g, bank):
                    pe.wait_ge(sl["negmax_ready"], g + 1)
                    pe.transpose(ps[0:SPL * 32, bank, 0:P // 2].bitcast(BF16),
                                 negmax[:, :, :].rearrange("p c n -> p (c n)"), identb[:, :])\
                        .then_inc(sl["negmaxT_psum"], 1)

                def out_turn(g, h, bank):
                    pe.wait_ge(sl["o_copied"], 2 * g + h + 1 + AT_ONE)
                    for k in range(4):
                        last = pe.transpose(ps[:, bank, k * P:(k + 1) * P], oT[:, k * P:(k + 1) * P], ident[:, :])
                    last.then_inc(sl["o_turned"], 1)

                def quad_loaded(b, q):
                    pe.wait_ge(loaded[l][q], 16 * QUAD_LOADS * (b + 1))

                quad_loaded(0, 0)
                for n in range(32):
                    pass_a(0, 0, n // 8, n % 8)
                quad_loaded(0, 1)
                for n in range(8):
                    if n == 2:
                        pe.wait_ge(sl["max_done"], 32 + 2)
                        negmax_turn(0, turn_bank(1))
                    if n == 3:
                        pe.wait_ge(sl["negmaxT_ready"], 1)
                    pass_a(1, 1, 0, n)

                def batch(b, final):
                    for q in range(4):
                        g = 4 * b + q
                        more_1, more_2 = not (final and q == 3), not (final and q >= 2)
                        pe.wait_ge(sl["negmax_rows"], 16 * (g + 1))
                        for ev in hd.events:
                            if ev[0] == "B":
                                pass_b(g, q, ev[1], ev[2])
                            elif ev[0] == "A":
                                k = ev[1]
                                if k == 0:
                                    for kind, h in hd.readers[32]:
                                        assert kind == "ON"
                                        pe.wait_ge(sl["attn_done"], 2 * g + h - 1 + AT_ONE)
                                if more_1:
                                    borrowed(k, g)
                                if k < 24 and more_1:
                                    pass_a(g + 1, (q + 1) % 4, 1 + k // 8, k % 8)
                                if k >= 24 and more_2:
                                    if k == 24:
                                        quad_loaded(b + (q >= 2), (q + 2) % 4)
                                    pass_a(g + 2, (q + 2) % 4, 0, k % 8)
                            elif ev[0] == "PV":
                                pv(g, q, ev[1])
                                if final and q == 3 and ev[1] in EARLY["tensor"][l]:
                                    pe.wait_ge(sl["max_done"], 32 * NQ)
                                    (prepare, ff_prepare)[l](*EARLY["tensor"][l][ev[1]], early=True)
                            elif ev[0] == "MT" and more_1:
                                free(ev[2], g)
                                pe.wait_ge(sl["attn_done"], 2 * g + ev[3] + AT_ONE)
                                negmax_turn(g + 1, turn_bank(ev[2]))
                            elif ev[0] == "OT":
                                free(ev[2], g)
                                pe.wait_ge(sl["attn_done"], 2 * g + ev[1] + AT_ONE)
                                pe.wait_ge(sl["negmaxT_ready"], g + 1 + (ev[3] if more_1 else 0))
                                out_turn(g, ev[1], turn_bank(ev[2]))

                pe.wait_ge(sl["rest_done"] if l == 0 else sl["qk_sb"], 2 * NG + AT_ONE)
                pe.wait_ge(sl["v_taken"], NG + AT_ONE)
                with pe.Fori(0, B - 1) as b:
                    batch(b, False)
                batch(B - 1, True)
                pe.wait_ge(sl["attn_done"], 2 * NQ + AT_ONE)

            def prepare(u, stage, early=False):
                first, second = (1, 3) if early else (6, 7)
                if stage == 0:
                    pe.wait_ge(pre["attn_staged"], u + 1)
                    pe.wait_ge(pre["h_ready"], u)
                    turn(tokens, first, pre["a_turned"])
                elif stage == 1:
                    pe.wait_ge(pre["a_ready"], u + 1)
                    pe.wait_ge(pre["weights"], u)
                    for k in range(GT):
                        last = pe.matmul(ps[:, second, k * D:(k + 1) * D], aT[:, k * P:(k + 1) * P], wo0[:, :],
                                         start=True, stop=True)
                    last.then_inc(pre["wo_out"], 1)
                elif stage == 2:
                    pe.wait_ge(pre["normed"], u + 1)
                    turn(tokens2, first, pre["turned"])
                else:
                    pe.wait_ge(pre["h_ready"], u + 1)
                    for k in range(GT):
                        last = pe.matmul(ps[:, second, k * E:(k + 1) * E], hT[:, k * P:(k + 1) * P], wr[:, :],
                                         start=True, stop=True)
                    last.then_inc(pre["logits"], 1)

            def gate_up(u, e):
                for c, (f, w) in enumerate(FCH):
                    n = 3 * (E * u + e) + c
                    par = (3 * e + c) % 2
                    moving = hT_all[:, bass.ts(u, GW)]
                    pe.wait_ge(moe["silu"], n + 1)
                    pe.matmul(ps[0:w, par, :], wg[:, e, f:f + w], moving,
                              start=True, stop=True).then_inc(moe["gate"], 1)
                    pe.wait_ge(moe["mul"], n + 1)
                    pe.matmul(ps[0:w, 2 + par, :], wu[:, e, f:f + w], moving,
                              start=True, stop=True).then_inc(moe["up"], 1)

            def down(u, e):
                n = E * u + e
                pe.wait_ge(moe["mul"], 3 * n + 5)
                pe.wait_ge(moe["acc"], n + 1)
                for k in range(GT):
                    for c, (f, w) in enumerate(FCH):
                        last = pe.matmul(ps[:, 4 + e % 2, k * D:(k + 1) * D],
                                         acts[0:w, e % 2, c, k * P:(k + 1) * P], wd[0:w, c, e, :],
                                         start=(c == 0), stop=(c == len(FCH) - 1))
                last.then_inc(moe["down"], 1)

            def experts(u, more):
                for e in range(E):
                    gate_up(u, e)
                    if e:
                        down(u, e - 1)
                    if more and e in (1, 2, 5, 6):
                        prepare(u + 1, (1, 2, 5, 6).index(e))
                down(u, E - 1)

            def ff_prepare(u, stage, early=False):
                first, second, third = (1, 3, 1) if early else (0, 1, 7)
                if stage == 0:
                    pe.wait_ge(ff["attn_staged"], u + 1)
                    if early and u > 0:
                        pe.wait_ge(ff["h_ready"], u)
                    turn(tokens, first, ff["a_turned"])
                elif stage == 1:
                    pe.wait_ge(ff["a_ready"], u + 1)
                    for k in range(GT):
                        pe.matmul(ps[:, second, k * D:(k + 1) * D], aT[:, k * P:(k + 1) * P], wo1[:, :],
                                  start=True, stop=False)
                        last = pe.matmul(ps[:, second, k * D:(k + 1) * D], aT[:, k * P:(k + 1) * P], ident[:, :],
                                         start=False, stop=True)
                    last.then_inc(ff["wo_out"], 1)
                else:
                    pe.wait_ge(ff["normed"], u + 1)
                    turn(tokens2, third, ff["turned"])

            def ff_hidden(u, c):
                if c == 0:
                    pe.wait_ge(ff["h_ready"], u + 1)
                if not isinstance(u, int) or u > 0:
                    pe.wait_ge(ff["hid"], FC * u + c + 1 - FC)
                pe.matmul(ps[:, 2 + c, :], w1[:, c * P:(c + 1) * P], hT_all[:, bass.ts(u, GW)],
                          start=True, stop=True).then_inc(ff["hidden"], 1)

            def ff_out(u, c):
                pe.wait_ge(ff["relu"], FC * u + c + 1)
                if c == 0:
                    pe.wait_ge(ff["y_ready"], u + AT_ONE)
                for k in range(GT):
                    last = pe.matmul(ps[:, 6, k * D:(k + 1) * D], act1[:, c, k * P:(k + 1) * P], w2[:, c, :],
                                     start=(c == 0 and k == 0), stop=(c == FC - 1), skip_group_check=True)
                last.then_inc(ff["y_out"], 1)

            def feed_forward(u, before=True, now=True, following=True, more=True):
                if now:
                    ff_hidden(u, 0)
                    ff_hidden(u, 1)
                if following:
                    ff_prepare(u + 1, 2)
                if more:
                    ff_prepare(u + 2, 0)
                if before:
                    ff_out(u - 1, 1)
                if now:
                    ff_hidden(u, 2)
                if more:
                    ff_prepare(u + 2, 1)
                if now:
                    ff_hidden(u, 3)
                if before:
                    ff_out(u - 1, 2)
                    ff_out(u - 1, 3)
                if now:
                    ff_out(u, 0)

            pe.wait_ge(consts, 5)
            pe.wait_ge(wqvk_in, 16)
            project(0)
            pe.wait_ge(w_in, 16 * len(weights))
            attention(0)
            with pe.Fori(0, NG - 1) as u:
                experts(u, True)
            experts(NG - 1, False)
            project(1)
            attention(1)
            feed_forward(0, before=False)
            with pe.Fori(0, NG - 3) as v:
                feed_forward(v + 1)
            feed_forward(NG - 2, more=False)
            feed_forward(NG - 1, following=False, more=False)
            feed_forward(NG, now=False, following=False, more=False)

        @block.scalar
        def _(act):
            act.dma_start(wqvk[:, :], Wqvk).then_inc(wqvk_in, 16)
            for dst, src in weights:
                act.dma_start(dst, src).then_inc(w_in, 16)
            act.sem_inc(moe["silu"], 2)
            for l in range(2):
                act.sem_inc(s[l]["exp_done"], 3)

            def project(l):
                sl = s[l]
                nh = H if l == 0 else KV
                rows = (P, P if l == 0 else KV * HD)

                def input_of(u, half):
                    h = (hT, aT)[half]
                    act.wait_ge(sl["turned"], u + 1)
                    if not isinstance(u, int) or u >= 2:
                        act.wait_ge(sl["v_out"], u - 1)
                    if l == 0:
                        act.activation(h[:, :], ps[:, 4 * half, :], ACT.Copy).then_inc(sl["h_ready"], 1)
                    else:
                        act.activation(h[:, :], ps[:, 4 * half, :], ACT.Copy, scale=gcol[:, 0:1])\
                            .then_inc(sl["h_ready"], 1)

                def body(v, half, more):
                    u = 2 * v + half
                    if not isinstance(v, int) or v > 0:
                        act.wait_ge(sl["parts_written"][half], 32 * v)
                    for n in range(2):
                        r = rows[n]
                        if l == 0:
                            act.wait_ge(sl[("q_out", "k_out")[n]], u + 1)
                            src = ps[0:r, 4 * half + 1 + n, :]
                        else:
                            act.wait_ge(sl["qk_sb"], 2 * u + n + 1 + AT_ONE)
                            src = qk32[0:r, n, :]
                        act.activation(parts[0:r, half, n, 0, :], src, ACT.Copy).then_inc(sl["hi_done"], 1)
                    act.wait_ge(sl["v_out"], u + 1)
                    act.activation(v1[:, bass.ts(u, GT), 0:nh * (HD + 1)]
                                   .rearrange("p t (h i) -> p t h i", i=HD + 1)[:, :, :, 0:HD],
                                   ps[:, 4 * half + 3, 0:GT * nh * HD].rearrange("p (t h i) -> p t h i", t=GT, i=HD),
                                   ACT.Copy).then_inc(sl["v_taken"], 1)
                    for n in range(2):
                        r = rows[n]
                        act.wait_ge(sl["rest_done"], 2 * u + n + 1 + AT_ONE)
                        act.activation(parts[0:r, half, n, 1, :], rest[0:r, n, :], ACT.Copy)\
                            .then_inc(sl["mid_done"], 1)
                    if more:
                        input_of(u + 2, half)

                for half in range(2):
                    input_of(half, half)
                for half in range(2):
                    body(0, half, True)
                with act.Fori(0, NG // 2 - 2) as v:
                    for half in range(2):
                        body(v + 1, half, True)
                for half in range(2):
                    body(NG // 2 - 1, half, False)

            def attention(l):
                sl, hd = s[l], LAYERS[l]
                G, nB = hd.G, 4 * hd.G

                def negmax_copy(g, bank):
                    act.wait_ge(sl["negmaxT_psum"], g + 1)
                    if not isinstance(g, int) or g > 0:
                        act.wait_ge(sl["negmax_rows"], 16 * g)
                    act.activation(negmaxT[:, :], ps[0:SPL * 32, bank, 0:P // 2].bitcast(BF16),
                                   ACT.Copy).then_inc(sl["negmaxT_ready"], 1)

                negmax_copy(0, turn_bank(1))

                def batch(b, final):
                    for q in range(4):
                        g = 4 * b + q
                        for ev in hd.events:
                            if ev[0] == "B":
                                m, j = ev[1], ev[2]
                                n = nB * g + 4 * m + j
                                c = hd.cols(m)
                                act.wait_ge(sl["scoresT"], n + 1)
                                if j == 0:
                                    act.wait_ge(sl["pv_done"], G * g + m + 1)
                                act.activation(probs[:, (4 * m + j) % PR, c:HALF], ps[:, B_BANKS[(4 * m + j) % 3], c:HALF],
                                               ACT.Exp, scale=SCALE).then_inc(sl["exp_done"], 1)
                            elif ev[0] == "OC":
                                act.wait_ge(sl["pv_done"], G * g + hd.last_of_half[ev[1]] + 3)
                                act.activation(oT[:, :], ps[:, PV_BANK, :], ACT.Copy)\
                                    .then_inc(sl["o_copied"], 1)
                            elif ev[0] == "PV" and final and q == 3 and ev[1] in EARLY["scalar"][l]:
                                (prepare, ff_prepare)[l](*EARLY["scalar"][l][ev[1]], early=True)
                            elif ev[0] == "MC" and not (final and q == 3):
                                negmax_copy(g + 1, turn_bank(ev[2]))

                with act.Fori(0, B - 1) as b:
                    batch(b, False)
                batch(B - 1, True)

            def prepare(u, stage, early=False):
                first = 1 if early else 6
                if stage == 0:
                    act.wait_ge(pre["a_turned"], u + 1)
                    act.activation(aT[:, :], ps[:, first, :], ACT.Copy).then_inc(pre["a_ready"], 1)
                elif stage == 2:
                    act.wait_ge(pre["turned"], u + 1)
                    act.wait_ge(pre["logits"], u)
                    act.activation(hT[:, :], ps[:, first, :], ACT.Copy)
                    act.activation(hT_all[:, bass.ts(u, GW)], ps[:, first, :], ACT.Copy).then_inc(pre["h_ready"], 1)
                elif stage == 3:
                    act.wait_ge(pre["shifted"], u + 1)
                    act.activation(rb[:, :, :], ra[:, :, :], ACT.Exp).then_inc(pre["exped"], 1)

            def experts(u, more):
                for e in range(E):
                    for c, (f, w) in enumerate(FCH):
                        n = 3 * (E * u + e) + c
                        par = (3 * e + c) % 2
                        act.wait_ge(moe["gate"], n + 1)
                        act.wait_ge(moe["mul"], n + 1)
                        act.activation(gated[0:w, par, :], ps[0:w, par, :], ACT.Silu).then_inc(moe["silu"], 1)
                    if more and e in (1, 5, 7):
                        prepare(u + 1, e // 2)
                    if not more and e == 4:
                        act.wait_ge(theta["reduced"], 1)
                        act.activation(sin_th[:, :], thr[:, :], ACT.Sin).then_inc(theta["sines"], 1)
                        act.activation(cos_th[:, :], thc[:, :], ACT.Sin).then_inc(theta["sines"], 1)

            def ff_prepare(u, stage, early=False):
                first, third = (1, 1) if early else (0, 7)
                if stage == 0:
                    act.wait_ge(ff["a_turned"], u + 1 + AT_ONE)
                    act.activation(aT[:, :], ps[:, first, :], ACT.Copy).then_inc(ff["a_ready"], 1)
                else:
                    act.wait_ge(ff["turned"], u + 1)
                    act.activation(hT_all[:, bass.ts(u, GW)], ps[:, third, :], ACT.Copy).then_inc(ff["h_ready"], 1)

            act.wait_ge(consts, 5)
            project(0)
            attention(0)
            with act.Fori(0, NG - 1) as u:
                experts(u, True)
            experts(NG - 1, False)
            project(1)
            attention(1)

            def hidden(u, c):
                act.wait_ge(ff["hidden"], FC * u + c + 1)
                if not isinstance(u, int) or u > 0:
                    act.wait_ge(ff["relu"], FC * u + c + 1 - FC)
                act.activation(arg[:, c, :], ps[:, 2 + c, :], ACT.Identity, bias=argb[:, c:c + 1],
                               scale=0.1 / TWO_PI).then_inc(ff["arg"], 1)
                act.activation(hid[:, c, :], ps[:, 2 + c, :], ACT.Identity, bias=b1c[:, c:c + 1])\
                    .then_inc(ff["hid"], 1)

            def sines(u, c):
                act.wait_ge(ff["reduced"], FC * u + c + 1)
                act.activation(arg[:, c, :], arg[:, c, :], ACT.Sin, scale=2.0 * PI_IN).then_inc(ff["sine"], 1)

            def relu(u, c):
                act.wait_ge(ff["mixed"], FC * u + c + 1)
                act.wait_ge(ff["y_out"], FC * u + c + 1)
                act.activation(act1[:, c, :], arg[:, c, :], ACT.Relu).then_inc(ff["relu"], 1)

            def feed_forward(u, before=True, now=True, following=True, more=True):
                for c in range(FC):
                    if now:
                        hidden(u, c)
                    if c == 1 and following:
                        ff_prepare(u + 1, 1)
                    if c == 1 and more:
                        ff_prepare(u + 2, 0)
                    if c and now:
                        sines(u, c - 1)
                    if c == 0 and before:
                        sines(u - 1, FC - 1)
                    if c >= 2 and now:
                        relu(u, c - 2)
                    if c < 2 and before:
                        relu(u - 1, c + 2)

            feed_forward(0, before=False)
            with act.Fori(0, NG - 3) as v:
                feed_forward(v + 1)
            feed_forward(NG - 2, more=False)
            feed_forward(NG - 1, following=False, more=False)
            feed_forward(NG, now=False, following=False, more=False)

        @block.vector
        def _(dve):
            own = Chain(dve, vec)
            dve.sem_inc(moe["mul"], 2)
            dve.memset(ones_rows(2, 4), TWO_ONES).then_inc(k_ones, 1)
            dve.sem_inc(moe["acc"], 2)
            for l in range(2):
                dve.sem_inc(s[l]["pv_done"], 2)

            def reduce_angle(dst, src):
                own.done(dve.tensor_scalar(tc1[:, :], src, 1.0 / TWO_PI, ROUND, ALU.mult, ALU.add))
                own.done(dve.tensor_scalar(tc1[:, :], tc1[:, :], ROUND, None, ALU.subtract))
                own.done(dve.scalar_tensor_tensor(tc2[:, :], tc1[:, :], -C1, src, ALU.mult, ALU.add))
                own.done(dve.scalar_tensor_tensor(tc2[:, :], tc1[:, :], -C2, tc2[:, :], ALU.mult, ALU.add))
                own.done(dve.tensor_scalar(dst, tc2[:, :], PI_IN, -PI_IN, ALU.min, ALU.max))

            def phases_terms():
                dve.wait_ge(w_in, 16 * len(weights))
                reduce_angle(thr[:, :], th[:, :])
                own.done(dve.tensor_scalar(thc[:, :], thr[:, :], float(np.pi / 2), None, ALU.add))
                own.done(dve.scalar_tensor_tensor(argb[:, :], b1c[:, :], 0.1, thr[:, :], ALU.mult, ALU.add))
                own.done(dve.tensor_scalar(argb[:, :], argb[:, :], 1.0 / TWO_PI, None, ALU.mult))
                reduce_angle(thc[:, :], thc[:, :])
                dve.tensor_copy(thc[:, :], thc[:, :]).then_inc(theta["reduced"], 1)

            def phases_coefficient():
                dve.wait_ge(theta["sines"], 2)
                own.done(dve.tensor_tensor(cos_th[:, :], cos_th[:, :], wrl[:, :], ALU.mult))
                own.done(dve.tensor_tensor(sin_th[:, :], sin_th[:, :], wim[:, :], ALU.mult))
                own.done(dve.tensor_tensor(cos_th[:, :], cos_th[:, :], sin_th[:, :], ALU.add))
                own.done(dve.scalar_tensor_tensor(coef[:, :], cos_th[:, :], 0.1, wim[:, :], ALU.mult, ALU.mult))

            def statistics(u, ready):
                apart(dve)
                for k in range(GT):
                    last = dve.bn_stats(stats[:, k, :], x[:, u * GT + k, :])
                own.done(last)
                apart(dve)
                for k in range(GT):
                    last = dve.bn_aggr(mv[:, k, :], stats[:, k, :])
                last.then_inc(ready, 1)

            def normalise(u, rstd_ready, dst, done):
                dve.wait_ge(rstd_ready, u + 1)
                for k in range(GT):
                    last = dve.tensor_scalar(dst[:, k, :], x[:, u * GT + k, :], mv[:, k, 0:1], rstd[:, k:k + 1],
                                             ALU.subtract, ALU.mult)
                last.then_inc(done, 1)

            def project(l):
                sl = s[l]
                rows = (P, P if l == 0 else KV * HD)
                def statistics_of_batch(b):
                    dve.wait_ge(x_in[b], 16)
                    apart(dve)
                    for k in range(BT):
                        last = dve.bn_stats(stats_b[:, k, :], x[:, b * BT + k, :])
                    own.done(last)
                    apart(dve)
                    for k in range(BT):
                        last = dve.bn_aggr(mv_all[:, b * BT + k, :], stats_b[:, k, :])
                    own.done(last)
                    dve.sem_inc(sl["stats_ready"], 1)

                def norm(u):
                    if l == 1:
                        dve.wait_ge(sl["rstd_ready"], u + 1 + AT_ONE)
                    elif isinstance(u, int) and u < 2:
                        dve.wait_ge(rstd_first, 1)
                    if not isinstance(u, int) or u > 0:
                        dve.wait_ge(sl["turned"], u)
                    for k in range(GT):
                        last = dve.tensor_scalar(tokens[:, k, :], x[:, u * GT + k, :], mv_all[:, u * GT + k, 0:1],
                                                 rstd_all[:, bass.ds(u * GT + k, 1)], ALU.subtract, ALU.mult)
                    last.then_inc(sl["normed"], 1)

                def body(u, half, more):
                    src = [ps[0:rows[n], 4 * half + 1 + n, :] for n in range(2)]
                    if l == 1:
                        for n, out_sem in enumerate(("q_out", "k_out")):
                            dve.wait_ge(sl[out_sem], u + 1)
                            dve.wait_ge(sl["rest_done"], 2 * u + AT_ONE)
                            dve.tensor_tensor(qk32[0:rows[n], n, :], src[n],
                                              ropeT[0:rows[n], half * GW:(half + 1) * GW],
                                              ALU.mult).then_inc(sl["qk_sb"], 1)
                            src[n] = qk32[0:rows[n], n, :]
                    if more:
                        norm(u + 2)
                    dve.wait_ge(sl["split_done"], 2 * u + AT_ONE)
                    for n in range(2):
                        dve.wait_ge(sl["hi_done"], 2 * u + n + 1)
                        dve.tensor_tensor(rest[0:rows[n], n, :], src[n], parts[0:rows[n], half, n, 0, :], ALU.subtract)\
                            .then_inc(sl["rest_done"], 1)
                    for n in range(2):
                        dve.wait_ge(sl["mid_done"], 2 * u + n + 1)
                        dve.tensor_tensor(parts[0:rows[n], half, n, 2, :], rest[0:rows[n], n, :],
                                          parts[0:rows[n], half, n, 1, :], ALU.subtract).then_inc(sl["split_done"], 1)

                if l == 0:
                    for b in range(B):
                        statistics_of_batch(b)
                norm(0)
                norm(1)
                if l == 0:
                    dve.wait_ge(sl["rstd_ready"], B - 1 + AT_ONE)
                with dve.Fori(0, NG // 2 - 1) as v:
                    for half in range(2):
                        body(2 * v + half, half, True)
                for half in range(2):
                    body(NG - 2 + half, half, False)

            def attention(l):
                sl, hd = s[l], LAYERS[l]

                def row_max(quad, j, i, par):
                    n = 32 * quad + 8 * j + i
                    dve.wait_ge(sl["scores"], n + 1)
                    dve.tensor_reduce(rowmax[:, par, 8 * j + i:8 * j + i + 1], score_a(i % 2)[:, 0:hd.keys(i)],
                                      AX, ALU.max).then_inc(sl["max_done"], 1)

                def negmax_split(g, par):
                    dve.wait_ge(sl["max_done"], 32 * g + 32)
                    if not isinstance(g, int) or g > 0:
                        dve.wait_ge(sl["negmaxT_psum"], g)
                    mx = rowmax[:, par, :]
                    own.done(dve.tensor_scalar(negmax[:, 0, :], mx, -1.0, None, ALU.mult))
                    own.done(dve.scalar_tensor_tensor(negrest[:, :], mx, -1.0, negmax[:, 0, :],
                                                      ALU.mult, ALU.subtract))
                    own.done(dve.tensor_copy(negmax[:, 1, :], negrest[:, :]))
                    dve.tensor_tensor(negmax[:, 2, :], negrest[:, :], negmax[:, 1, :], ALU.subtract)\
                        .then_inc(sl["negmax_ready"], 1)

                def normalise_out(g, b, q, h, bank):
                    dve.wait_ge(sl["o_turned"], 2 * g + h + 1 + AT_ONE)
                    o = ps[:, bank, :].rearrange("p (k j c) -> p k j c", k=4, c=32)
                    own.done(dve.reciprocal(rden[:, :, :], o[:, :, :, HD]))
                    dst = attn[:, bass.ds(8 * b + 4 * h, 4), :]
                    dst = dst.rearrange("p k (a c i) -> p k a c i", a=4, c=4)
                    dst = dst[:, :, q, :, :] if l == 0 else dst[:, :, :, q, :]
                    dve.tensor_tensor(dst, o[:, :, :, 0:HD], rden[:, :, :].unsqueeze(3).broadcast_to([P, 4, 4, HD]),
                                      ALU.mult).then_inc(sl["attn_done"], 1)

                for n in range(32):
                    row_max(0, n // 8, n % 8, 0)
                negmax_split(0, 0)
                for n in range(8):
                    row_max(1, 0, n, 1)

                def batch(b, final):
                    for q in range(4):
                        g = 4 * b + q
                        more_1, more_2 = not (final and q == 3), not (final and q >= 2)
                        for ev in hd.events:
                            if ev[0] == "A":
                                k = ev[1]
                                if k < 24 and more_1:
                                    row_max(g + 1, 1 + k // 8, k % 8, (q + 1) % 2)
                                if k >= 24 and more_2:
                                    row_max(g + 2, 0, k % 8, q % 2)
                                if k == 23 and more_1:
                                    negmax_split(g + 1, (q + 1) % 2)
                            elif ev[0] == "PV" and final and q == 3 and ev[1] in EARLY["vector"][l]:
                                dve.wait_ge(sl["attn_done"], 2 * 4 + AT_ONE)
                                (prepare, ff_prepare)[l](*EARLY["vector"][l][ev[1]], early=True)
                            elif ev[0] == "ON":
                                normalise_out(g, b, q, ev[1], turn_bank(ev[2]))

                per = 4 * (3 + 2)
                with dve.Fori(0, B - 1) as b:
                    own.loop(b, per)
                    batch(b, False)
                own.end_loop(B - 1, per)
                batch(B - 1, True)

            def over_e(a):
                return a.unsqueeze(2).broadcast_to([P, GT, E])

            def prepare(u, stage, early=False):
                second = 3 if early else 7
                if stage == 0:
                    dve.tensor_copy(tokens[:, :, :], attn[:, bass.ts(u, GT), :]).then_inc(pre["attn_staged"], 1)
                elif stage == 1:
                    dve.wait_ge(pre["wo_out"], u + 1)
                    xs = x[:, bass.ts(u, GT), :]
                    own.done(dve.tensor_tensor(xs, xs, ps[:, second, :].rearrange("p (t d) -> p t d", t=GT), ALU.add))
                    statistics(u, pre["stats"])
                elif stage == 2:
                    dve.wait_ge(pre["stats"], u + 1)
                    normalise(u, pre["rstd"], tokens2, pre["normed"])
                elif stage == 3:
                    dve.wait_ge(pre["logits"], u + 1)
                    lg = ps[:, second, 0:GT * E].rearrange("p (t e) -> p t e", t=GT)
                    own.done(dve.tensor_reduce(r1[:, :], lg, AX, ALU.max))
                    dve.tensor_tensor(ra[:, :, :], lg, over_e(r1[:, :]), ALU.subtract).then_inc(pre["shifted"], 1)
                else:
                    dve.wait_ge(pre["exped"], u + 1)
                    own.done(dve.tensor_reduce(r1[:, :], rb[:, :, :], AX, ALU.add))
                    own.done(dve.reciprocal(r2[:, :], r1[:, :]))
                    own.done(dve.tensor_tensor(rb[:, :, :], rb[:, :, :], over_e(r2[:, :]), ALU.mult))
                    mine = rb[:, :, :].unsqueeze(3).broadcast_to([P, GT, E, E])
                    other = rb[:, :, :].unsqueeze(2).broadcast_to([P, GT, E, E])
                    dve.tensor_tensor(cmp1[:, :, :, :], other, mine, ALU.is_gt)
                    own.done(dve.tensor_tensor(cmp2[:, :, :, :], other, mine, ALU.is_equal))
                    own.done(dve.tensor_tensor(cmp2[:, :, :, :], cmp2[:, :, :, :],
                                               lower[:, :, :].unsqueeze(1).broadcast_to([P, GT, E, E]), ALU.mult))
                    own.done(dve.tensor_tensor(cmp1[:, :, :, :], cmp1[:, :, :, :], cmp2[:, :, :, :], ALU.add))
                    dve.tensor_reduce(ra[:, :, :], cmp1[:, :, :, :], AX, ALU.add).then_inc(pre["ranked"], 1)

            def expert_weights(u):
                dve.wait_ge(pre["ranked"], u + 1)
                own.done(dve.scalar_tensor_tensor(rc[:, :, :], ra[:, :, :], 2.0, rb[:, :, :],
                                                  ALU.is_lt, ALU.mult))
                own.done(dve.tensor_reduce(r1[:, :], rc[:, :, :], AX, ALU.add))
                own.done(dve.reciprocal(r2[:, :], r1[:, :]))
                dve.tensor_tensor(ew[:, bass.ts(u, GT), :], rc[:, :, :], over_e(r2[:, :]), ALU.mult)\
                    .then_inc(pre["weights"], 1)

            def multiply(u, e):
                for c, (f, w) in enumerate(FCH):
                    n = 3 * (E * u + e) + c
                    par = (3 * e + c) % 2
                    if c == 0 and e:
                        dve.wait_ge(moe["down"], E * u + e - 1 + AT_ONE)
                    dve.wait_ge(moe["silu"], n + 3)
                    dve.wait_ge(moe["up"], n + 1)
                    dve.tensor_tensor(acts[0:w, e % 2, c, :], ps[0:w, 2 + par, :], gated[0:w, par, :], ALU.mult)\
                        .then_inc(moe["mul"], 1)

            def accumulate(u, e):
                n = E * u + e
                dve.wait_ge(moe["down"], n + 1 + AT_ONE)
                dve.wait_ge(moe["acc"], n + 2)
                if e == 0:
                    dve.wait_ge(pre["weights"], u + 1)
                for k in range(GT):
                    xs = x[:, u * GT + k, :]
                    last = dve.scalar_tensor_tensor(xs, ps[:, 4 + e % 2, k * D:(k + 1) * D],
                                                    ew[:, u * GT + k, e:e + 1], xs, ALU.mult, ALU.add)
                last.then_inc(moe["acc"], 1)

            def statistics_rms(u):
                dve.wait_ge(s[1]["rstd_ready"], u + AT_ONE)
                dve.wait_ge(moe["acc"], E * u + E + 2)
                apart(dve)
                for k in range(GT):
                    last = dve.bn_stats(stats[:, k, :], x[:, u * GT + k, :])
                own.done(last)
                apart(dve)
                for k in range(GT):
                    last = dve.bn_aggr(mv1[:, k, :], stats[:, k, :])
                own.done(last)
                dve.tensor_copy(mv_all[:, bass.ts(u, GT), :], mv1[:, :, :]).then_inc(s[1]["stats_ready"], 1)

            def experts(u, more):
                for e in range(E):
                    multiply(u, e)
                    if e == 1:
                        expert_weights(u)
                    if e:
                        accumulate(u, e - 1)
                    if more and e in (0, 3, 4, 6):
                        prepare(u + 1, (0, 3, 4, 6).index(e))
                    if e == 0:
                        prepare(u, 4)
                    if not more and e == 2:
                        phases_terms()
                    if not more and e == 6:
                        phases_coefficient()
                accumulate(u, E - 1)
                statistics_rms(u)

            def ff_prepare(u, stage, early=False):
                second = 3 if early else 1
                if stage == 0:
                    dve.wait_ge(ff["a_turned"], u + AT_ONE)
                    dve.tensor_copy(tokens[:, :, :], attn[:, bass.ts(u, GT), :]).then_inc(ff["attn_staged"], 1)
                elif stage == 1:
                    xs = x[:, bass.ts(u, GT), :]
                    dve.wait_ge(ff["wo_out"], u + 1)
                    own.done(dve.tensor_tensor(xs, xs, ps[:, second, :].rearrange("p (t d) -> p t d", t=GT), ALU.add))
                    statistics(u, ff["stats"])
                else:
                    dve.wait_ge(ff["stats"], u + 1)
                    if not isinstance(u, int) or u > 0:
                        dve.wait_ge(ff["turned"], u)
                    normalise(u, ff["rstd"], tokens2, ff["normed"])

            project(0)
            attention(0)
            dve.wait_ge(s[0]["attn_done"], 2 * NQ + AT_ONE)
            chain = 2 + 10 + 2
            with dve.Fori(0, NG - 1) as u:
                own.loop(u, chain)
                experts(u, True)
            own.end_loop(NG - 1, chain)
            experts(NG - 1, False)
            dve.wait_ge(moe["acc"], E * NG + 2)
            project(1)
            attention(1)
            dve.wait_ge(s[1]["attn_done"], 2 * NQ + AT_ONE)

            def reduced(u, c):
                dve.wait_ge(ff["turns"], FC * u + c + 1)
                dve.tensor_tensor(arg[:, c, :], arg[:, c, :], turns[:, c, :], ALU.subtract)\
                    .then_inc(ff["reduced"], 1)

            def mixed(u, c):
                dve.wait_ge(ff["sine"], FC * u + c + 1)
                a = arg[:, c, :]
                dve.scalar_tensor_tensor(a, a, coef[:, c:c + 1], hid[:, c, :], ALU.mult, ALU.add)\
                    .then_inc(ff["mixed"], 1)

            def finish(u):
                dve.wait_ge(ff["y_out"], FC * u + 2 * FC)
                dve.wait_ge(ff["added"], u + 1)
                dve.tensor_tensor(y[:, :, :], y[:, :, :], ps[:, 6, :].rearrange("p (t d) -> p t d", t=GT),
                                  ALU.add).then_inc(ff["y_ready"], 1)

            def feed_forward(u, before=True, now=True, following=True, more=True):
                for c in range(FC):
                    if c and now:
                        reduced(u, c - 1)
                    if c == 0 and before:
                        reduced(u - 1, FC - 1)
                    if c >= 2 and now:
                        mixed(u, c - 2)
                    if c < 2 and before:
                        mixed(u - 1, c + 2)
                    if c != 1 and more:
                        ff_prepare(u + 2, max(0, c - 1))
                    if c == 2 and before:
                        finish(u - 1)

            feed_forward(0, before=False)
            with dve.Fori(0, NG - 3) as v:
                own.loop(v, 2)
                feed_forward(v + 1)
            own.end_loop(NG - 3, 2)
            feed_forward(NG - 2, more=False)
            feed_forward(NG - 1, following=False, more=False)
            feed_forward(NG, now=False, following=False, more=False)


_INS = ["L0_attn_h", "L0_attn_Wqvk", "L0_attn_Wo", "L0_ffn_router_w", "L0_ffn_gate_proj", "L0_ffn_up_proj",
        "L0_ffn_down_proj", "L1_attn_w_q", "L1_attn_w_k", "L1_attn_w_v", "L1_attn_w_o", "L1_attn_g", "L1_ffn_W1",
        "L1_ffn_b1", "L1_ffn_quantum_phases", "L1_ffn_quantum_weights_real", "L1_ffn_quantum_weights_imag",
        "L1_ffn_W2", "L1_ffn_b2"]


def rope_table():
    i = np.arange(HD)
    theta = np.power(np.float32(10000.0), (-2.0 * (i // 2) / HD).astype(np.float32))
    angle = np.arange(S, dtype=np.float32)[:, None] * theta[None, :]
    sign = np.where(np.arange(S) % 2 == 1, -1.0, 1.0).astype(np.float32)
    factor = np.cos(angle) + sign[:, None] * np.sin(angle)
    return np.ascontiguousarray(np.tile(factor.T, (H, 1)), dtype=np.float32)


_COLUMNS = {"L1_attn_g", "L1_ffn_b1", "L1_ffn_quantum_phases", "L1_ffn_quantum_weights_real",
            "L1_ffn_quantum_weights_imag"}


def kernel(**inputs):
    import concourse.bacc as bacc
    from concourse.bass_utils import run_bass_kernel_spmd

    nc = bacc.Bacc("TRN2", target_bir_lowering=False, num_devices=1)
    arrays, args = {}, []
    for name, a in [(n, inputs[n]) for n in _INS] + [("rope", rope_table())]:
        a = np.asarray(a)
        a = np.ascontiguousarray(a.reshape(-1, P).T if name in _COLUMNS else a)
        arrays[f"in_{name}_dram"] = a
        args.append(nc.dram_tensor(f"in_{name}_dram", a.shape, mybir.dt.from_np(a.dtype), kind="ExternalInput").ap())
    out = nc.dram_tensor("out_0_dram", (B, S, D), F32, kind="ExternalOutput").ap()
    build(nc, *args, out)
    r = run_bass_kernel_spmd(nc, [arrays], core_ids=[0])
    return r.results[0]["out_0_dram"]
```
